# Optimizing a Trainium2 kernel written in Bass

```python
import numpy as np
import jax
import jax.numpy as jnp

def _softmax(x, axis=-1):
    return jax.nn.softmax(x, axis=axis)

def _gelu(x):
    return jax.nn.gelu(x, approximate=True)

def _silu(x):
    return jax.nn.silu(x)

def _sigmoid(x):
    return jax.nn.sigmoid(x)

def _layernorm(x, axis=-1, eps=1e-05):
    m = jnp.mean(x, axis=axis, keepdims=True)
    v = jnp.var(x, axis=axis, keepdims=True)
    return (x - m) / jnp.sqrt(v + eps)

def _scatter_add(tgt, idx, src, axis=0):
    return tgt.at[idx].add(src)

def _segment_sum(src, seg, n):
    return jax.ops.segment_sum(src, seg, n)
kernel_name = 'mk_adj_preln_d1_adj_r2_2fc3c0'

def setup_inputs(seed: int=0):
    np.random.seed(seed)
    _w = jnp.asarray

    def _rec_inputs():
        import jax
        import jax.numpy as jnp
        _gk = jax.random.key(seed)
        x = -0.0005146 + 1 * jax.random.normal(jax.random.fold_in(_gk, 1), (8, 1024, 128), jnp.float32)
        _w = (1.0 + jnp.arange(1024, dtype=jnp.float32)) ** (-0.5)
        _w = _w / _w.mean()
        _pij = jnp.clip(0.0078125 * _w[:, None] * _w[None, :], 0.0, 1.0)
        _a = jax.random.uniform(jax.random.fold_in(_gk, 2), (8, 1024, 1024)) < _pij
        adj = _a.astype(jnp.int32)
        return (x, adj)
    x, adj = _rec_inputs()

    def _L0_gnn_setup():
        import jax, jax.numpy as jnp
        import numpy as np
        B, N, C, OUT, S = (4, 1024, 128, 128, 25)
        DENSITY = 0.008
        key = jax.random.key(seed)
        kA, kX, kW = jax.random.split(key, 3)
        A = jax.random.bernoulli(kA, DENSITY, (B, N, N)).astype(jnp.int32)
        X = jax.random.normal(kX, (B, N, C), dtype=jnp.float32)
        W = jax.random.normal(kW, (2 * C, OUT), dtype=jnp.float32) * np.float32(1.0 / np.sqrt(2 * C))
        b = jnp.zeros((OUT,), dtype=jnp.float32)
        return {'A': A, 'X': X, 'W': W, 'b': b}
    _L0_gnn_all = _L0_gnn_setup()
    _L0_gnn_in = {k: v for k, v in _L0_gnn_all.items() if k in ('W', 'b')}
    del _L0_gnn_all
    return {'x': x, 'adj': adj, 'L0_gnn_W': _L0_gnn_in['W'], 'L0_gnn_b': _L0_gnn_in['b']}

def reference(x, adj, L0_gnn_W, L0_gnn_b):
    import jax
    import jax.numpy as jnp

    def _L0_gnn_ref(A, X, W, b):
        import jax, jax.numpy as jnp
        import numpy as np
        B, N, C, OUT, S = (4, 1024, 128, 128, 25)
        DENSITY = 0.008
        mask = A != 0
        neg_inf = jnp.float32(-jnp.inf)
        pri = -jnp.arange(N, dtype=jnp.float32)
        scores = jnp.where(mask, pri, neg_inf)
        vals, idx = jax.lax.top_k(scores, S)
        valid = vals > neg_inf
        feats = jax.vmap(lambda x, i: x[i])(X, idx)
        feats = jnp.where(valid[..., None], feats, neg_inf)
        agg = feats.max(axis=2)
        degree = mask.sum(axis=-1)
        agg = jnp.where((degree <= S)[..., None], jnp.maximum(agg, 0.0), agg)
        h = jnp.concatenate([X, agg], axis=-1)
        out = jax.nn.relu(jnp.einsum('bnf,fo->bno', h, W) + b)
        return out
    h = jnp.maximum(_layernorm(x, axis=-1), 0.0)
    x = x + _L0_gnn_ref(adj, h, L0_gnn_W, L0_gnn_b)
    return x

_drawn_inputs = setup_inputs


def setup_inputs(seed=0):
    import zlib

    import numpy as np

    out = dict(_drawn_inputs(seed))
    spreads = {'L0_gnn_b': (0.0, 0.1)}
    factors = {}
    for name, (base, spread) in spreads.items():
        noise = np.random.default_rng([zlib.crc32(name.encode()), seed]).standard_normal(out[name].shape)
        drawn = base * np.exp(spread * noise) if base else spread * noise
        out[name] = jnp.asarray(drawn.astype(out[name].dtype))
    for name, factor in factors.items():
        out[name] = (out[name] * factor).astype(out[name].dtype)
    return out
```

```python
from contextlib import ExitStack, nullcontext

import concourse.bass as bass
from concourse import mybir

F32 = mybir.dt.float32
BF16 = mybir.dt.bfloat16
I32 = mybir.dt.int32
ALU = mybir.AluOpType
ACT = mybir.ActivationFunctionType
AX = mybir.AxisListType


def gnn_layer(nc, x, adj, w, bias, out):
    P = 128
    NBATCH, N, C = x.shape
    OUT = w.shape[1]
    Q = N // P
    TILES = N // P
    SAMPLES = 25
    EPS = 1e-5
    PARTS = 3
    MARK = 128.0
    MIN_LEVELS = 3
    KVALS = 32
    SLOTS = 4
    PAIRS = NBATCH // 2
    LAST = PAIRS - 1
    N_CONSTS = 11

    x_v = x.rearrange("b (p q) c -> b p (q c)", q=Q)
    out_v = out.rearrange("b (p q) c -> b p (q c)", q=Q)
    adj_v = adj.rearrange("b (t p) j -> b t p j", p=P)

    ctx = ExitStack()
    with ctx:
        def sb(name, shape, dt):
            return ctx.enter_context(nc.sbuf_tensor(name, shape, dt))

        def ps(name, shape, dt):
            return ctx.enter_context(nc.psum_tensor(name, shape, dt))

        def sem(name):
            return ctx.enter_context(nc.semaphore(name))

        ident_b = sb("ident_b", [P, P], BF16)
        ident_f = sb("ident_f", [P, P], F32)
        rank_w = sb("rank_w", [P, P], BF16)
        ones_row = sb("ones_row", [P, N], BF16)
        level_val = sb("level_val", [P, KVALS], F32)
        half = sb("half", [P, Q], F32)
        w_sb = sb("w_sb", [P, 2, OUT], F32)
        bias_row = sb("bias_row", [1, OUT], F32)
        ones_f = sb("ones_f", [1, P], F32)
        adj_in = sb("adj_in", [P, SLOTS, N], I32)
        sign = sb("sign", [P, 2, N], BF16)
        mask = sb("mask", [P, 2, TILES, N], BF16)
        degree = sb("degree", [P, 2, TILES], F32)
        degree_all = sb("degree_all", [P, 2, TILES], F32)
        degree_int = sb("degree_int", [P, 2, TILES], I32)
        prefix = sb("prefix", [P, N], BF16)
        mask_t = sb("mask_t", [P, 2, Q, P], BF16)
        rank = sb("rank", [P, 2, TILES, Q * P], BF16)
        count_max = sb("count_max", [P, 2, TILES], F32)
        count_all = sb("count_all", [P, 2, TILES], F32)
        levels_int = sb("levels_int", [P, 2, TILES], I32)
        x_in = sb("x_in", [P, 2, Q, C], F32)
        x_skip = sb("x_skip", [P, 2, Q, C], F32)
        trash = sb("trash", [P, Q, C], BF16)
        neg_mean = sb("neg_mean", [P, Q], F32)
        sq_sum = sb("sq_sum", [P, Q], F32)
        var_eps = sb("var_eps", [P, Q], F32)
        rstd = sb("rstd", [P, Q], F32)
        h_norm = sb("h_norm", [P, Q, C], F32)
        h = sb("h", [P, 2, Q, C], F32)
        h_parts = sb("h_parts", [P, 2, PARTS, Q, C], BF16)
        h_rest = sb("h_rest", [P, Q, C], F32)
        h_t = sb("h_t", [P, 2, Q, P], F32)
        onehot = sb("onehot", [P, 2, Q, P], BF16)
        level_top = sb("level_top", [P, 2, P], F32)
        agg = sb("agg", [P, 2, N], F32)
        relu = sb("relu", [P, Q, OUT], F32)
        y = sb("y", [P, 2, Q, OUT], F32)

        gathered = ps("gathered", [P, 2, Q, P], F32)
        mask_tp = ps("mask_tp", [P, Q, P], BF16)
        rank_ps = ps("rank_ps", [P, Q, P], F32)
        misc = ps("misc", [P, 512], F32)
        counts = misc[:, 0:TILES * Q].rearrange("p (t q) -> p t q", q=Q)

        def projection():
            return misc[:, P:P + OUT]

        s_passed = {e: sem("passed_" + e) for e in ("SP", "Activation", "Pool", "DVE", "PE")}
        s_consts = sem("consts")
        s_weights = sem("weights")
        s_x = [sem(f"x_loaded{k}") for k in range(2)]
        s_skip = [sem(f"x_skip_loaded{k}") for k in range(2)]
        s_adj = [sem(f"adj_loaded{k}") for k in range(SLOTS)]
        s_stored = [sem(f"stored{k}") for k in range(2)]
        s_signed = sem("signed")
        s_masked = sem("masked")
        s_deg_all = sem("degree_all_done")
        s_deg_int = sem("degree_int_done")
        s_capped = sem("capped")
        s_transposed = sem("mask_transposed")
        s_mask_t = sem("mask_t_copied")
        s_ranked = sem("ranked")
        s_counted = sem("counted")
        s_rank_sb = sem("rank_copied")
        s_cmax = sem("count_max_done")
        s_call = sem("count_all_done")
        s_levels = sem("levels_known")
        s_mean = sem("neg_mean_done")
        s_sq = sem("sq_sum_done")
        s_var = sem("var_done")
        s_rstd = sem("rstd_done")
        s_norm = sem("h_norm_done")
        s_h = sem("h_done")
        s_hi = sem("h_hi_done")
        s_rest = sem("h_rest_done")
        s_mid = sem("h_mid_done")
        s_lo = sem("h_lo_done")
        s_h_tp = sem("h_transposed")
        s_h_t = sem("h_t_copied")
        s_onehot = sem("onehot_ready")
        s_gathered = sem("level_gathered")
        s_top = sem("level_top_done")
        s_agg = sem("agg_ready")
        s_proj = sem("projected")
        s_relu = sem("relu_done")
        s_y = sem("y_ready")

        block = ctx.enter_context(nc.Block())

        def number(pair, par):
            return 2 * pair + par

        def following(pair, par):
            return (pair, 1) if par == 0 else (pair + 1, 0)

        def previous(pair, par):
            return (pair, 0) if par == 1 else (pair - 1, 1)

        def where(eng, cond):
            return nullcontext() if cond is True else eng.If(cond)

        def earlier(n):
            return n if type(n) is int else n & 0xFFFF

        def wait_alone(eng, semaphore, value):
            eng.wait_ge(semaphore, value)
            if type(value) is not int:
                eng.sem_inc(s_passed[eng.engine.name], 1)

        def has_next(pair, par):
            return True if par == 0 else pair < LAST

        def has_second_next(pair, par):
            return pair < LAST

        def has_previous(pair, par):
            return True if par == 1 else pair > 0

        @block.sync
        def _(sp):
            def existing(b):
                return b if type(b) is int else nc.s_assert_within(
                    b, 0, NBATCH - 1, skip_runtime_bounds_check_because="the loop's branches bound it")

            def load_x(pair, par):
                sp.dma_start(x_in[:, par, :, :].rearrange("p q c -> p (q c)"),
                             x_v[existing(number(pair, par))]).then_inc(s_x[par], 16)

            def load_tile(b, t):
                sp.dma_start(adj_in[:, t % SLOTS, :], adj_v[existing(b), t]).then_inc(s_adj[t % SLOTS], 16)

            for t in range(SLOTS):
                load_tile(0, t)
            load_x(0, 0)
            sp.dma_start(w_sb[:, :, :], w.rearrange("(g p) o -> p g o", p=P)).then_inc(s_weights, 16)
            sp.dma_start(bias_row[:, :], bias.rearrange("(a o) -> a o", a=1)).then_inc(s_weights, 16)
            load_x(0, 1)
            for u in range(SLOTS, 2 * TILES):
                sp.wait_ge(s_signed, u - SLOTS + 1)
                load_tile(u // TILES, u % TILES)
            with sp.Fori(0, PAIRS) as pair:
                for par in range(2):
                    b = number(pair, par)
                    with where(sp, pair > 0):
                        wait_alone(sp, s_y, earlier(b - 1))
                    sp.dma_start(x_skip[:, par, :, :].rearrange("p q c -> p (q c)"),
                                 x_v[b]).then_inc(s_skip[par], 16)
                    with where(sp, has_second_next(pair, par)):
                        wait_alone(sp, s_norm, b + 1)
                        load_x(pair + 1, par)
                        for t in range(TILES):
                            wait_alone(sp, s_signed, TILES * (b + 2) + t - SLOTS + 1)
                            load_tile(b + 2, t)
                    with where(sp, has_previous(pair, par)):
                        sp.wait_ge(s_y, earlier(b))
                        sp.dma_start(out_v[existing(b - 1)], y[:, 1 - par, :, :].rearrange("p q c -> p (q c)")
                                     ).then_inc(s_stored[1 - par], 16)
            sp.wait_ge(s_y, NBATCH)
            sp.dma_start(out_v[NBATCH - 1], y[:, 1, :, :].rearrange("p q c -> p (q c)")).then_inc(s_stored[1], 16)
            for par in range(2):
                sp.wait_ge(s_stored[par], 16 * PAIRS)

        @block.scalar
        def _(act):
            def mask_tile(pair, par, t):
                act.wait_ge(s_adj[t % SLOTS], 16 * (TILES // SLOTS * number(pair, par) + t // SLOTS + 1))
                nc.scalar.activation(sign[:, t % 2, :], adj_in[:, t % SLOTS, :], ACT.Sign).then_inc(s_signed, 1)
                act.wait_ge(s_signed, TILES * number(pair, par) + t + 1)
                nc.scalar.activation(mask[:, par, t, :], sign[:, t % 2, :], ACT.Square,
                                     accum_out=degree[:, par, t:t + 1]).then_inc(s_masked, 1)

            def mask_t_copy(b, t, first=False):
                u = TILES * b + t
                if not first:
                    act.wait_ge(s_counted, u - 1)
                act.wait_ge(s_transposed, u + 1)
                nc.scalar.activation(mask_t[:, t % 2, :, :], mask_tp[:, :, :], ACT.Copy).then_inc(s_mask_t, 1)

            def rank_copy(b, par, t):
                act.wait_ge(s_ranked, TILES * b + t + 1)
                nc.scalar.activation(rank[:, par, t, :], rank_ps[:, :, :].rearrange("p q n -> p (q n)"),
                                     ACT.Copy).then_inc(s_rank_sb, 1)

            def norm_stats(pair, par):
                act.wait_ge(s_x[par], 16 * (pair + 1))
                for q in range(Q):
                    last = nc.scalar.activation(trash[:, q, :], x_in[:, par, q, :], ACT.Copy, scale=-1.0 / C,
                                                accum_out=neg_mean[:, q:q + 1])
                last.then_inc(s_mean, 1)
                act.wait_ge(s_mean, number(pair, par) + 1)
                for q in range(Q):
                    last = nc.scalar.activation(trash[:, q, :], x_in[:, par, q, :], ACT.Square,
                                                bias=neg_mean[:, q:q + 1], accum_out=sq_sum[:, q:q + 1])
                last.then_inc(s_sq, 1)

            def h_and_hi(b, par):
                act.wait_ge(s_norm, b + 1)
                nc.scalar.activation(h[:, par, :, :], h_norm[:, :, :], ACT.Relu).then_inc(s_h, 1)
                act.wait_ge(s_h, b + 1)
                nc.scalar.activation(h_parts[:, par, 0, :, :], h[:, par, :, :], ACT.Copy).then_inc(s_hi, 1)

            def h_mid(b, par):
                act.wait_ge(s_rest, b + 1)
                nc.scalar.activation(h_parts[:, par, 1, :, :], h_rest[:, :, :], ACT.Copy).then_inc(s_mid, 1)

            def relu_copy(b, s):
                act.wait_ge(s_proj, earlier(TILES * b + s + 1))
                nc.scalar.activation(relu[:, s, :], projection(), ACT.Relu).then_inc(s_relu, 1)

            for t in range(TILES):
                mask_tile(0, 0, t)
            norm_stats(0, 0)
            for t in range(TILES):
                mask_t_copy(0, t, first=t < 2)
                if t >= 1:
                    rank_copy(0, 0, t - 1)
                if t == 2:
                    h_and_hi(0, 0)
                if t == 5:
                    h_mid(0, 0)
            rank_copy(0, 0, TILES - 1)
            for t in range(TILES):
                mask_tile(0, 1, t)
            with act.Fori(0, PAIRS) as pair:
                for par in range(2):
                    b = number(pair, par)
                    act.wait_ge(s_h_tp, b + 1)
                    nc.scalar.activation(h_t[:, par, :, :], rank_ps[:, :, :], ACT.Copy).then_inc(s_h_t, 1)
                    with where(act, has_next(pair, par)):
                        norm_stats(*following(pair, par))
                    with where(act, has_previous(pair, par)):
                        wait_alone(act, s_agg, earlier(b))
                    for s in range(TILES):
                        with where(act, has_next(pair, par)):
                            mask_t_copy(b + 1, s)
                        with where(act, has_second_next(pair, par)):
                            mask_tile(pair + 1, par, s)
                        with where(act, has_next(pair, par)):
                            rank_copy(b + 1, 1 - par, s)
                            if s == 2:
                                h_and_hi(b + 1, 1 - par)
                            if s == 5:
                                h_mid(b + 1, 1 - par)
                        if s == 0:
                            with where(act, pair > 0):
                                wait_alone(act, s_y, earlier(b - 1))
                        with where(act, has_previous(pair, par)):
                            relu_copy(b - 1, s)
            act.wait_ge(s_y, NBATCH - 1)
            for s in range(TILES):
                relu_copy(NBATCH - 1, s)

        @block.gpsimd
        def _(pool):
            nc.gpsimd.memset(ident_b[:, :], 0.0).then_inc(s_consts, 1)
            nc.gpsimd.memset(ident_f[:, :], 0.0).then_inc(s_consts, 1)
            nc.gpsimd.memset(rank_w[:, :], 1.0).then_inc(s_consts, 1)
            nc.gpsimd.memset(ones_row[:, :], 1.0).then_inc(s_consts, 1)
            nc.gpsimd.memset(ones_f[:, :], 1.0).then_inc(s_consts, 1)
            nc.gpsimd.memset(half[:, :], -0.5).then_inc(s_consts, 1)
            nc.gpsimd.iota(level_val[:, :], pattern=[[1, KVALS]], base=int(MARK), channel_multiplier=0,
                           allow_small_or_imprecise_dtypes=True).then_inc(s_consts, 1)
            wait_alone(pool, s_consts, 7)
            for m in (ident_b, ident_f):
                nc.gpsimd.affine_select(out=m[:, :], in_=m[:, :], compare_op=ALU.not_equal, fill=1.0, base=0,
                                        pattern=[[-1, P]], channel_multiplier=1).then_inc(s_consts, 1)
            nc.gpsimd.affine_select(out=rank_w[:, :], in_=rank_w[:, :], compare_op=ALU.is_gt, fill=0.0, base=0,
                                    pattern=[[1, P]], channel_multiplier=-1).then_inc(s_consts, 1)
            wait_alone(pool, s_consts, 10)
            nc.gpsimd.affine_select(out=rank_w[:, :], in_=rank_w[:, :], compare_op=ALU.not_equal, fill=MARK,
                                    base=0, pattern=[[1, P]], channel_multiplier=-1).then_inc(s_consts, 1)
            all_max = bass.bass_isa.ReduceOp.max

            def degrees(b, par):
                wait_alone(pool, s_masked, TILES * b + TILES)
                nc.gpsimd.partition_all_reduce(degree_all[:, par, :], degree[:, par, :], P, all_max
                                               ).then_inc(s_deg_all, 1)
                wait_alone(pool, s_deg_all, b + 1)
                nc.gpsimd.tensor_copy(degree_int[:, par, :], degree_all[:, par, :]).then_inc(s_deg_int, 1)

            def levels(b, par):
                wait_alone(pool, s_cmax, b + 1)
                nc.gpsimd.partition_all_reduce(count_all[:, par, :], count_max[:, par, :], P, all_max
                                               ).then_inc(s_call, 1)
                wait_alone(pool, s_call, b + 1)
                nc.gpsimd.tensor_copy(levels_int[:, par, :], count_all[:, par, :]).then_inc(s_levels, 1)

            def normalise(b, par):
                wait_alone(pool, s_sq, b + 1)
                nc.gpsimd.tensor_scalar(var_eps[:, :], sq_sum[:, :], 1.0 / C, EPS, ALU.mult, ALU.add
                                        ).then_inc(s_var, 1)
                wait_alone(pool, s_var, b + 1)
                nc.gpsimd.tensor_tensor(rstd[:, :], var_eps[:, :], half[:, :], ALU.pow).then_inc(s_rstd, 1)
                wait_alone(pool, s_rstd, b + 1)
                for q in range(Q):
                    last = nc.gpsimd.tensor_scalar(h_norm[:, q, :], x_in[:, par, q, :], neg_mean[:, q:q + 1],
                                                   rstd[:, q:q + 1], ALU.add, ALU.mult)
                last.then_inc(s_norm, 1)

            def split(b, par):
                wait_alone(pool, s_hi, b + 1)
                nc.gpsimd.tensor_tensor(h_rest[:, :, :], h[:, par, :, :], h_parts[:, par, 0, :, :],
                                        ALU.subtract).then_inc(s_rest, 1)
                wait_alone(pool, s_mid, b + 1)
                nc.gpsimd.tensor_tensor(h_parts[:, par, 2, :, :], h_rest[:, :, :], h_parts[:, par, 1, :, :],
                                        ALU.subtract).then_inc(s_lo, 1)

            def add_skip(pair, par):
                wait_alone(pool, s_relu, earlier(TILES * number(pair, par) + TILES))
                wait_alone(pool, s_skip[par], earlier(16 * (pair + 1)))
                nc.gpsimd.tensor_tensor(y[:, par, :, :], relu[:, :, :], x_skip[:, par, :, :], ALU.add
                                        ).then_inc(s_y, 1)

            degrees(0, 0)
            normalise(0, 0)
            split(0, 0)
            levels(0, 0)
            degrees(1, 1)
            with pool.Fori(0, PAIRS) as pair:
                for par in range(2):
                    b = number(pair, par)
                    with where(pool, has_next(pair, par)):
                        normalise(b + 1, 1 - par)
                        split(b + 1, 1 - par)
                    with where(pool, has_previous(pair, par)):
                        before, _ = previous(pair, par)
                        with where(pool, before > 0):
                            wait_alone(pool, s_stored[1 - par], earlier(16 * before))
                        add_skip(*previous(pair, par))
                    with where(pool, has_next(pair, par)):
                        levels(b + 1, 1 - par)
                    with where(pool, has_second_next(pair, par)):
                        degrees(b + 2, par)
            wait_alone(pool, s_stored[1], 16 * (PAIRS - 1))
            add_skip(PAIRS - 1, 1)

        def load_counts(engine, counts_int, least, most):
            return nc.values_load_multi_w_load_instructions(
                counts_int, engines=[engine.engine], min_val=least, max_val=most,
                skip_runtime_bounds_check_because="a row has at most N neighbours")[1]

        @block.vector
        def _(dve):
            level = dve.alloc_register("levels_folded")
            dve.reg_mov(level, 0)

            def cap(b, par):
                wait_alone(dve, s_deg_int, b + 1)
                largest = load_counts(nc.vector, degree_int[0:1, par, :], 0, N)
                for t in range(TILES):
                    with dve.If(largest[t] > SAMPLES):
                        nc.vector.tensor_tensor_scan(prefix[:, :], ones_row[:, :], mask[:, par, t, :], 0.0,
                                                     ALU.mult, ALU.add)
                        dve.drain()
                        nc.vector.scalar_tensor_tensor(mask[:, par, t, :], prefix[:, :], float(SAMPLES),
                                                       mask[:, par, t, :], ALU.is_le, ALU.mult)
                        dve.drain()

            def make_onehot(par, t, k, buf):
                nc.vector.tensor_scalar(onehot[:, bass.ds(buf, 1), :, :].rearrange("p a q n -> p (a q n)"),
                                        rank[:, par, t, :], level_val[:, bass.ds(k, 1)], None,
                                        ALU.is_equal).then_inc(s_onehot, 1)

            def fold_level(par, t, ahead):
                now = dve.snap(level)
                buf = dve.snap(now % 2)
                dve.wait_ge(s_gathered, now + 1)
                nc.vector.tensor_reduce(level_top[:, bass.ds(buf, 1), :].rearrange("p a n -> p (a n)"),
                                        gathered[:, bass.ds(buf, 1), :, :].rearrange("p a q n -> p (a n) q"),
                                        AX.X, ALU.max).then_inc(s_top, 1)
                if ahead is not None:
                    make_onehot(par, *ahead, buf)
                dve.wait_ge(s_top, now + 1)
                here = agg[:, par, P * t:P * (t + 1)]
                last = nc.vector.tensor_tensor(here, here,
                                               level_top[:, bass.ds(buf, 1), :].rearrange("p a n -> p (a n)"),
                                               ALU.max)
                dve.reg_add(level, level, 1)
                return last

            def count_maxima(b, par):
                dve.wait_ge(s_counted, TILES * b + TILES)
                nc.vector.tensor_reduce(count_max[:, par, :], counts, AX.X, ALU.max)
                dve.drain()
                nc.vector.tensor_scalar(count_max[:, par, :], count_max[:, par, :], float(MIN_LEVELS), None,
                                        ALU.max).then_inc(s_cmax, 1)

            dve.wait_ge(s_consts, N_CONSTS)
            cap(0, 0)
            nc.vector.memset(agg[:, 0, :], 0.0).then_inc(s_capped, 1)
            count_maxima(0, 0)
            with dve.Fori(0, PAIRS) as pair:
                for par in range(2):
                    b = number(pair, par)
                    with where(dve, has_next(pair, par)):
                        cap(b + 1, 1 - par)
                    with where(dve, pair > 0):
                        wait_alone(dve, s_proj, earlier(TILES * (b - 1)))
                    nc.vector.memset(agg[:, par, :], 0.0).then_inc(s_capped, 1)
                    wait_alone(dve, s_rank_sb, TILES * b + TILES)
                    wait_alone(dve, s_levels, b + 1)
                    n_levels = list(load_counts(nc.vector, levels_int[0:1, par, :], MIN_LEVELS, SAMPLES))
                    odd = dve.snap(sum(n_levels[1:], n_levels[0]) % 2)
                    n_levels[-1] = dve.snap(n_levels[-1] + odd)
                    make_onehot(par, 0, 0, 0)
                    make_onehot(par, 0, 1, 1)
                    wait_alone(dve, s_capped, b + 2)
                    for t in range(TILES):
                        with dve.Fori(0, n_levels[t] - 2) as k:
                            fold_level(par, t, (t, k + 2))
                        for k in range(2):
                            last = fold_level(par, t, (t + 1, k) if t + 1 < TILES else None)
                    last.then_inc(s_agg, 1)
                    with where(dve, has_next(pair, par)):
                        with where(dve, has_previous(pair, par)):
                            wait_alone(dve, s_relu, earlier(TILES * b))
                        count_maxima(b + 1, 1 - par)

        @block.tensor
        def _(pe):
            level = pe.alloc_register("levels_gathered")
            pe.reg_mov(level, 0)

            def transpose_tile(b, par, t, first=False):
                if not first:
                    pe.wait_ge(s_mask_t, TILES * b + t)
                for q in range(Q):
                    last = nc.tensor.transpose(mask_tp[:, q, :], mask[:, par, t, q:N:Q], ident_b[:, :])
                last.then_inc(s_transposed, 1)

            def rank_tile(b, t):
                u = TILES * b + t
                pe.wait_ge(s_mask_t, u + 1)
                for g in range(2):
                    last = nc.tensor.matmul(rank_ps[:, g * Q // 2:(g + 1) * Q // 2, :], rank_w[:, :],
                                            mask_t[:, t % 2, g * Q // 2:(g + 1) * Q // 2, :], start=True, stop=True)
                last.then_inc(s_ranked, 1)
                for q in range(Q):
                    last = nc.tensor.matmul(counts[:, t, q:q + 1], mask_t[:, t % 2, q, :], ones_row[:, 0:1],
                                            start=True, stop=True)
                last.then_inc(s_counted, 1)

            def project(b, par, s):
                o = projection()
                nc.tensor.matmul(o, ones_f[:, :], bias_row[:, :], start=True, stop=False)
                nc.tensor.matmul(o, h_t[:, par, s, :], w_sb[:, 0, :], start=False, stop=False)
                nc.tensor.matmul(o, agg[:, par, s:N:Q], w_sb[:, 1, :], start=False, stop=True).then_inc(s_proj, 1)

            def gather_level(par, buf, now):
                pe.wait_ge(s_onehot, now + buf + 1)
                for q in range(Q):
                    for part in range(PARTS):
                        last = nc.tensor.matmul(gathered[:, buf, q, :], h_parts[:, par, part, q, :],
                                                onehot[:, buf, q, :], start=(part == 0), stop=(part == PARTS - 1))
                last.then_inc(s_gathered, 1)

            pe.wait_ge(s_consts, N_CONSTS)
            pe.wait_ge(s_capped, 1)
            for t in range(TILES):
                transpose_tile(0, 0, t, first=t == 0)
                if t >= 1:
                    if t >= 2:
                        pe.wait_ge(s_rank_sb, t - 1)
                    rank_tile(0, t - 1)
            pe.wait_ge(s_rank_sb, TILES - 1)
            rank_tile(0, TILES - 1)
            pe.wait_ge(s_weights, 32)
            with pe.Fori(0, PAIRS) as pair:
                for par in range(2):
                    b = number(pair, par)
                    pe.wait_ge(s_h, b + 1)
                    pe.wait_ge(s_rank_sb, TILES * b + TILES)
                    for q in range(Q):
                        last = nc.tensor.transpose(rank_ps[:, q, :], h[:, par, q, :], ident_f[:, :])
                    last.then_inc(s_h_tp, 1)
                    with where(pe, has_next(pair, par)):
                        wait_alone(pe, s_capped, b + 2)
                    wait_alone(pe, s_lo, b + 1)
                    wait_alone(pe, s_levels, b + 1)
                    n_levels = load_counts(nc.tensor, levels_int[0:1, par, :], MIN_LEVELS, SAMPLES)
                    n_pairs = pe.snap((sum(n_levels[1:], n_levels[0]) + 1) // 2)
                    for s in range(TILES):
                        with where(pe, has_next(pair, par)):
                            transpose_tile(b + 1, 1 - par, s)
                        with pe.Fori(n_pairs * s // TILES, n_pairs * (s + 1) // TILES):
                            now = pe.snap(level)
                            for buf in range(2):
                                gather_level(par, buf, now)
                            pe.reg_add(level, level, 2)
                        with where(pe, pair > 0 if s == 0 else has_previous(pair, par)):
                            wait_alone(pe, s_relu, earlier(TILES * (b - 1) + s))
                        if s == 0:
                            wait_alone(pe, s_cmax, b + 1)
                        with where(pe, has_next(pair, par)):
                            if s == 0:
                                pe.wait_ge(s_h_t, b + 1)
                            else:
                                pe.wait_ge(s_rank_sb, TILES * (b + 1) + s)
                            rank_tile(b + 1, s)
                        with where(pe, has_previous(pair, par)):
                            if s == 0:
                                pe.wait_ge(s_agg, earlier(b))
                            project(b - 1, 1 - par, s)
            pe.wait_ge(s_agg, NBATCH)
            pe.wait_ge(s_h_t, NBATCH)
            for s in range(TILES):
                pe.wait_ge(s_relu, TILES * (NBATCH - 1) + s)
                project(NBATCH - 1, 1, s)


def kernel(x, adj, L0_gnn_W, L0_gnn_b):
    import numpy as np
    import concourse.bacc as bacc
    from concourse import mybir
    from concourse.bass_utils import run_bass_kernel_spmd

    nc = bacc.Bacc("TRN2", target_bir_lowering=False, num_devices=1)
    arrays, args = {}, []
    for name, a in (("x", x), ("adj", adj), ("w", L0_gnn_W), ("bias", L0_gnn_b)):
        a = np.ascontiguousarray(a)
        arrays[name] = a
        args.append(nc.dram_tensor(name, a.shape, mybir.dt.from_np(a.dtype), kind="ExternalInput").ap())
    args.append(nc.dram_tensor("out", arrays["x"].shape, mybir.dt.float32, kind="ExternalOutput").ap())
    gnn_layer(nc, *args)
    result = run_bass_kernel_spmd(nc, [arrays], core_ids=[0])
    return result.results[0]["out"]
```

```python
from contextlib import ExitStack, nullcontext

import concourse.bass as bass
from concourse import mybir

F32 = mybir.dt.float32
BF16 = mybir.dt.bfloat16
I32 = mybir.dt.int32
ALU = mybir.AluOpType
ACT = mybir.ActivationFunctionType
AX = mybir.AxisListType


def gnn_layer(nc, x, adj, w, bias, out):
    P = 128
    NBATCH, N, C = x.shape
    OUT = w.shape[1]
    Q = N // P
    TILES = N // P
    ALL_TILES = NBATCH * TILES
    SAMPLES = 25
    EPS = 1e-5
    PARTS = 3
    MARK = 128.0
    RING = 3
    MIN_LEVELS = RING + 1
    TOPS = 4
    KVALS = 32
    SLOTS = 4
    MASKS = 8
    LEAD = 4
    FIRST = TILES + 1
    GROUP = 32
    HALF = Q // 2
    H_PIECES = 4
    H_PIECE = Q // H_PIECES
    MIDDLE = (NBATCH - 2) // 2
    LAST = NBATCH - 1
    BIAS_ROWS = (0, 32, 64)
    N_CONSTS = 13

    x_v = x.rearrange("b (p q) c -> b p (q c)", q=Q)
    out_v = out.rearrange("b (p q) c -> b p (q c)", q=Q)
    adj_v = adj.rearrange("b (t p) j -> b t p j", p=P)

    ctx = ExitStack()
    with ctx:
        def sb(name, shape, dt):
            return ctx.enter_context(nc.sbuf_tensor(name, shape, dt))

        def ps(name, shape, dt):
            return ctx.enter_context(nc.psum_tensor(name, shape, dt))

        def sem(name):
            return ctx.enter_context(nc.semaphore(name))

        ident_b = sb("ident_b", [P, P], BF16)
        ident_f = sb("ident_f", [P, P], F32)
        rank_w = sb("rank_w", [P, P], BF16)
        ones = sb("ones", [P, N], BF16)
        level_val = sb("level_val", [P, KVALS], F32)
        half = sb("half", [P, Q], F32)
        w_sb = sb("w_sb", [P, 2, OUT], F32)
        bias_rows = sb("bias_rows", [P, OUT], F32)
        bias_hi = sb("bias_hi", [P, OUT], BF16)
        bias_rest = sb("bias_rest", [P, OUT], F32)
        bias_mid = sb("bias_mid", [P, OUT], BF16)
        bias_lo = sb("bias_lo", [P, OUT], BF16)
        bias_parts = sb("bias_parts", [P, OUT], BF16)
        adj_in = sb("adj_in", [P, SLOTS, N], I32)
        sign = sb("sign", [P, 2, N], BF16)
        mask = sb("mask", [P, MASKS, N], BF16)
        degree = sb("degree", [P, MASKS], F32)
        degree_all = sb("degree_all", [P, MASKS], F32)
        degree_int = sb("degree_int", [P, MASKS], I32)
        in_group = sb("in_group", [P, 2, N // GROUP, GROUP], BF16)
        of_groups = sb("of_groups", [P, 2, N // GROUP], F32)
        position = sb("position", [P, N // GROUP, GROUP], F32)
        kept = sb("kept", [P, N], BF16)
        prefix = sb("prefix", [P, N], BF16)
        mask_t = sb("mask_t", [P, 2, Q, P], BF16)
        rank = sb("rank", [P, 2, TILES, Q * P], BF16)
        counts = sb("counts", [P, 2, TILES, Q + 1], F32)
        count_max = sb("count_max", [P, 2, TILES], F32)
        count_all = sb("count_all", [P, 2, TILES], F32)
        levels_int = sb("levels_int", [P, 2, TILES], I32)
        x_in = sb("x_in", [P, 2, Q, C], F32)
        x_skip = sb("x_skip", [P, 2, Q, C], F32)
        trash = sb("trash", [P, Q, C], BF16)
        neg_mean = sb("neg_mean", [P, Q], F32)
        sq_sum = sb("sq_sum", [P, Q], F32)
        var_eps = sb("var_eps", [P, Q], F32)
        rstd = sb("rstd", [P, Q], F32)
        h_norm = sb("h_norm", [P, Q, C], F32)
        h = sb("h", [P, 2, Q, C], F32)
        h_parts = sb("h_parts", [P, 2, PARTS, Q, C], BF16)
        h_rest = sb("h_rest", [P, Q, C], F32)
        h_t = sb("h_t", [P, 2, Q, P], F32)
        onehot = sb("onehot", [P, RING, Q, P], BF16)
        level_top = sb("level_top", [P, TOPS, P], F32)
        agg = sb("agg", [P, 2, N], F32)
        relu = sb("relu", [P, Q, OUT], F32)
        y = sb("y", [P, 2, Q, OUT], F32)

        gathered = ps("gathered", [P, RING, Q, P], F32)
        bank_a = ps("bank_a", [P, 512], F32)
        bank_b = ps("bank_b", [P, 512], F32)
        mask_tp = bank_a[:, :].bitcast(BF16).rearrange("p (q n) -> p q n", q=Q)
        projection = bank_a[:, 0:OUT]
        counts_ps = bank_a[:, OUT:OUT + Q]
        first_counts_ps = bank_b[:, 0:Q]

        s_passed = {e: sem("passed_" + e) for e in ("SP", "Activation", "Pool", "DVE", "PE")}
        s_consts = sem("consts")
        s_weights = sem("weights")
        s_bias = sem("bias_loaded")
        s_bias_parts = sem("bias_parts_done")
        s_x = [sem(f"x_loaded{k}") for k in range(2)]
        s_skip = [sem(f"x_skip_loaded{k}") for k in range(2)]
        s_adj = [sem(f"adj_loaded{k}") for k in range(SLOTS)]
        s_stored = [sem(f"stored{k}") for k in range(2)]
        s_first_masked = sem("first_masked")
        s_signed = sem("signed")
        s_masked = sem("masked")
        s_deg_all = sem("degree_all_done")
        s_deg_int = sem("degree_int_done")
        s_capped = sem("capped")
        s_transposed = sem("mask_transposed")
        s_mask_t = sem("mask_t_copied")
        s_ranked = sem("ranked")
        s_rank_sb = sem("rank_copied")
        s_counted = sem("counted")
        s_counts_sb = sem("counts_copied")
        s_cmax = sem("count_max_done")
        s_call = sem("count_all_done")
        s_levels = sem("levels_known")
        s_mean = sem("neg_mean_done")
        s_sq = sem("sq_sum_done")
        s_var = sem("var_done")
        s_rstd = sem("rstd_done")
        s_norm = sem("h_norm_done")
        s_h = sem("h_done")
        s_hi = sem("h_hi_done")
        s_rest = sem("h_rest_done")
        s_mid = sem("h_mid_done")
        s_lo = sem("h_lo_done")
        s_h_tp = sem("h_transposed")
        s_h_t = sem("h_t_copied")
        s_onehot = sem("onehot_ready")
        s_gathered = sem("level_gathered")
        s_agg = sem("agg_ready")
        s_proj = sem("projected")
        s_relu = sem("relu_done")
        s_y = sem("y_ready")
        s_last_y = sem("last_y_ready")

        block = ctx.enter_context(nc.Block())

        def over_graphs(eng, graph):
            graph(0, 0, 0, None)
            with eng.Fori(0, MIDDLE) as pair:
                graph(2 * pair + 1, 1, pair, pair)
                graph(2 * pair + 2, 0, pair + 1, pair)
            graph(LAST, 1, LAST // 2, None)

        def where(eng, cond):
            return nullcontext() if cond is True else eng.If(cond)

        def wait_alone(eng, semaphore, value):
            eng.wait_ge(semaphore, value)
            if type(value) is not int:
                eng.sem_inc(s_passed[eng.engine.name], 1)

        def is_first(b):
            return type(b) is int and b == 0

        def is_last(b):
            return type(b) is int and b == LAST

        def tile_exists(par, pair, b, t):
            if t < TILES or pair is None:
                return True
            return True if par == 1 else pair < MIDDLE - 1

        def masks_made(first, t):
            if not first or t >= LEAD:
                return [t + LEAD]
            return range(2 * t + 1, min(2 * t + 3, 2 * LEAD))

        @block.sync
        def _(sp):
            def existing(b):
                return b if type(b) is int else nc.s_assert_within(
                    b, 0, NBATCH - 1, skip_runtime_bounds_check_because="the loop's branches bound it")

            def load_x(b, par):
                sp.dma_start(x_in[:, par, :, :].rearrange("p q c -> p (q c)"),
                             x_v[existing(b)]).then_inc(s_x[par], 16)

            def load_tile(b, t):
                sp.dma_start(adj_in[:, t % SLOTS, :], adj_v[existing(b), t]).then_inc(s_adj[t % SLOTS], 16)

            def store(b, par):
                sp.dma_start(out_v[existing(b)], y[:, par, :, :].rearrange("p q c -> p (q c)")
                             ).then_inc(s_stored[par], 16)

            load_x(0, 0)
            for t in range(SLOTS):
                load_tile(0, t)
            sp.dma_start(w_sb[:, :, :], w.rearrange("(g p) o -> p g o", p=P)).then_inc(s_weights, 16)
            sp.wait_ge(s_consts, N_CONSTS)
            for row in BIAS_ROWS:
                sp.dma_start(bias_rows[row:row + 1, :], bias.rearrange("(a o) -> a o", a=1)).then_inc(s_bias, 16)
            for u in range(SLOTS, FIRST + SLOTS):
                sp.wait_ge(s_first_masked, u - SLOTS + 1)
                load_tile(u // TILES, u % TILES)
                if u == TILES - 1:
                    load_x(1, 1)
            for u in range(FIRST + SLOTS, TILES + SLOTS + LEAD):
                sp.wait_ge(s_signed, u - SLOTS - FIRST + 1)
                load_tile(u // TILES, u % TILES)

            def graph(b, par, rnd, pair):
                if pair is not None:
                    with where(sp, pair > 0 if par == 1 else True):
                        wait_alone(sp, s_y, b - 1)
                elif is_last(b):
                    sp.wait_ge(s_y, b - 1)
                sp.dma_start(x_skip[:, par, :, :].rearrange("p q c -> p (q c)"),
                             x_v[b]).then_inc(s_skip[par], 16)
                if not is_last(b):
                    with where(sp, tile_exists(par, pair, b, TILES)):
                        wait_alone(sp, s_norm, b + 1)
                        load_x(b + 2, par)
                    for t in range(LEAD + SLOTS, LEAD + SLOTS + TILES):
                        with where(sp, tile_exists(par, pair, b, t)):
                            wait_alone(sp, s_signed, TILES * (b + 1) + t - SLOTS - FIRST + 1)
                            load_tile(b + 1 + t // TILES, t % TILES)
                if not is_first(b):
                    sp.wait_ge(s_y, b)
                    store(b - 1, 1 - par)

            over_graphs(sp, graph)
            for g in range(2):
                sp.wait_ge(s_last_y, HALF * (g + 1))
                sp.dma_start(out_v[LAST, :, g * HALF * C:(g + 1) * HALF * C],
                             y[:, 1, g * HALF:(g + 1) * HALF, :].rearrange("p q c -> p (q c)")
                             ).then_inc(s_stored[1], 16)
            sp.wait_ge(s_stored[0], 16 * (NBATCH // 2))
            sp.wait_ge(s_stored[1], 16 * (NBATCH // 2 + 1))

        @block.scalar
        def _(act):
            def mask_tile(b, t, rounds):
                u = TILES * b + t
                act.wait_ge(s_adj[t % SLOTS], 16 * (rounds + 1))
                nc.scalar.activation(sign[:, t % 2, :], adj_in[:, t % SLOTS, :], ACT.Sign).then_inc(s_signed, 1)
                act.wait_ge(s_signed, u - FIRST + 1)
                nc.scalar.activation(mask[:, t % MASKS, :], sign[:, t % 2, :], ACT.Square,
                                     accum_out=degree[:, t:t + 1]).then_inc(s_masked, 1)

            def mask_t_copy(u, t):
                act.wait_ge(s_transposed, u + 1)
                nc.scalar.activation(mask_t[:, t % 2, :, :], mask_tp, ACT.Copy).then_inc(s_mask_t, 1)

            def rank_copy(u, par, t, g):
                act.wait_ge(s_ranked, 2 * u + g + 1)
                nc.scalar.activation(rank[:, par, t, g * HALF * P:(g + 1) * HALF * P], bank_b[:, :],
                                     ACT.Copy).then_inc(s_rank_sb, 1)

            def counts_copy(u, par, t, source):
                act.wait_ge(s_counted, u + 1)
                nc.scalar.activation(counts[:, par, t, 0:Q], source, ACT.Copy).then_inc(s_counts_sb, 1)

            def means(b, par, rnd, blocks):
                act.wait_ge(s_x[par], 16 * (rnd + 1))
                for q in blocks:
                    last = nc.scalar.activation(trash[:, q, :], x_in[:, par, q, :], ACT.Copy, scale=-1.0 / C,
                                                accum_out=neg_mean[:, q:q + 1])
                if Q - 1 in blocks:
                    last.then_inc(s_mean, 1)

            def squares(b, par, blocks):
                act.wait_ge(s_mean, b + 1)
                for q in blocks:
                    last = nc.scalar.activation(trash[:, q, :], x_in[:, par, q, :], ACT.Square,
                                                bias=neg_mean[:, q:q + 1], accum_out=sq_sum[:, q:q + 1])
                if Q - 1 in blocks:
                    last.then_inc(s_sq, 1)

            def h_relu(b, par):
                act.wait_ge(s_norm, b + 1)
                nc.scalar.activation(h[:, par, :, :], h_norm[:, :, :], ACT.Relu).then_inc(s_h, 1)

            def h_hi(b, par):
                act.wait_ge(s_h, b + 1)
                nc.scalar.activation(h_parts[:, par, 0, :, :], h[:, par, :, :], ACT.Copy).then_inc(s_hi, 1)

            def h_mid(b, par):
                act.wait_ge(s_rest, b + 1)
                nc.scalar.activation(h_parts[:, par, 1, :, :], h_rest[:, :, :], ACT.Copy).then_inc(s_mid, 1)

            def h_t_copy(b, par, t):
                act.wait_ge(s_h_tp, H_PIECES * b + t + 1)
                nc.scalar.activation(h_t[:, par, t * H_PIECE:(t + 1) * H_PIECE, :],
                                     bank_b[:, 0:H_PIECE * P], ACT.Copy).then_inc(s_h_t, 1)

            def relu_copy(b, s):
                act.wait_ge(s_proj, TILES * b + s + 1)
                nc.scalar.activation(relu[:, s, :], projection, ACT.Relu).then_inc(s_relu, 1)

            means(0, 0, 0, range(Q))
            squares(0, 0, range(Q))
            for t in range(TILES + 1):
                if t < TILES:
                    mask_t_copy(t, t)
                if t >= 1:
                    act.wait_ge(s_ranked, 2 * t)
                    nc.scalar.activation(rank[:, 0, t - 1, :],
                                         gathered[:, (t - 1) % RING, :, :].rearrange("p q n -> p (q n)"),
                                         ACT.Copy).then_inc(s_rank_sb, 2)
                    counts_copy(t - 1, 0, t - 1, first_counts_ps)
                if t == 2:
                    h_relu(0, 0)
                    h_hi(0, 0)
                if t == 4:
                    h_mid(0, 0)
            def graph(b, par, rnd, pair):
                first, last = is_first(b), is_last(b)
                for t in range(TILES):
                    u = TILES * (b + 1) + t
                    if not last:
                        mask_t_copy(u, t)
                    if t < H_PIECES:
                        h_t_copy(b, par, t)
                    if not last:
                        for g in range(2):
                            rank_copy(u, 1 - par, t, g)
                    if not first:
                        if t == 0:
                            act.wait_ge(s_levels, b + 1)
                        relu_copy(b - 1, t)
                    if last:
                        continue
                    counts_copy(u, 1 - par, t, counts_ps)
                    for ahead in masks_made(first, t):
                        with where(act, tile_exists(par, pair, b, ahead)):
                            mask_tile(b + 1 + ahead // TILES, ahead % TILES,
                                      TILES // SLOTS * (b + 1) + ahead // SLOTS)
                    if t == 0:
                        means(b + 1, 1 - par, rnd + par, range(0, 6))
                    elif t == 1:
                        means(b + 1, 1 - par, rnd + par, range(6, Q))
                        squares(b + 1, 1 - par, range(0, HALF))
                    elif t == 2:
                        squares(b + 1, 1 - par, range(HALF, Q))
                    elif t == 3:
                        h_relu(b + 1, 1 - par)
                        h_hi(b + 1, 1 - par)
                    elif t == 4:
                        h_mid(b + 1, 1 - par)

            over_graphs(act, graph)

        def normalise(api, eng, b, par):
            wait_alone(eng, s_rstd, b + 1)
            for q in range(Q):
                last = api.tensor_scalar(h_norm[:, q, :], x_in[:, par, q, :], neg_mean[:, q:q + 1],
                                         rstd[:, q:q + 1], ALU.add, ALU.mult)
            last.then_inc(s_norm, 1)

        def split_rest(api, eng, b, par):
            wait_alone(eng, s_hi, b + 1)
            api.tensor_tensor(h_rest[:, :, :], h[:, par, :, :], h_parts[:, par, 0, :, :],
                              ALU.subtract).then_inc(s_rest, 1)

        def split_lo(api, eng, b, par):
            wait_alone(eng, s_mid, b + 1)
            api.tensor_tensor(h_parts[:, par, 2, :, :], h_rest[:, :, :], h_parts[:, par, 1, :, :],
                              ALU.subtract).then_inc(s_lo, 1)

        def last_projection(s):
            if s < 2 * RING:
                return gathered[:, s // 2, HALF * (s % 2), :]
            return (bank_a, bank_b)[s - 2 * RING][:, 0:OUT]

        def load_numbers(engine, numbers, least, most):
            return nc.values_load_multi_w_load_instructions(
                numbers, engines=[engine.engine], min_val=least, max_val=most,
                skip_runtime_bounds_check_because="a row has at most N neighbours")[1]

        @block.gpsimd
        def _(pool):
            nc.gpsimd.memset(bias_rows[:, :], 0.0).then_inc(s_consts, 1)
            nc.gpsimd.memset(bias_parts[:, :], 0.0).then_inc(s_consts, 1)
            nc.gpsimd.memset(counts[:, :, :, :], float(MIN_LEVELS)).then_inc(s_consts, 1)
            nc.gpsimd.memset(ident_b[:, :], 0.0).then_inc(s_consts, 1)
            nc.gpsimd.memset(ident_f[:, :], 0.0).then_inc(s_consts, 1)
            nc.gpsimd.memset(rank_w[:, :], 1.0).then_inc(s_consts, 1)
            nc.gpsimd.memset(ones[:, :], 1.0).then_inc(s_consts, 1)
            nc.gpsimd.memset(half[:, :], -0.5).then_inc(s_consts, 1)
            nc.gpsimd.iota(level_val[:, :], pattern=[[1, KVALS]], base=int(MARK), channel_multiplier=0,
                           allow_small_or_imprecise_dtypes=True).then_inc(s_consts, 1)
            wait_alone(pool, s_consts, 9)
            for m in (ident_b, ident_f):
                nc.gpsimd.affine_select(out=m[:, :], in_=m[:, :], compare_op=ALU.not_equal, fill=1.0, base=0,
                                        pattern=[[-1, P]], channel_multiplier=1).then_inc(s_consts, 1)
            nc.gpsimd.affine_select(out=rank_w[:, :], in_=rank_w[:, :], compare_op=ALU.is_gt, fill=0.0, base=0,
                                    pattern=[[1, P]], channel_multiplier=-1).then_inc(s_consts, 1)
            wait_alone(pool, s_consts, 12)
            nc.gpsimd.affine_select(out=rank_w[:, :], in_=rank_w[:, :], compare_op=ALU.not_equal, fill=MARK,
                                    base=0, pattern=[[1, P]], channel_multiplier=-1).then_inc(s_consts, 1)
            all_max = bass.bass_isa.ReduceOp.max

            def largest_degree(u, k):
                nc.gpsimd.partition_all_reduce(degree_all[:, k:k + 1], degree[:, k:k + 1], P, all_max
                                               ).then_inc(s_deg_all, 1)
                wait_alone(pool, s_deg_all, u + 1)
                nc.gpsimd.tensor_copy(degree_int[:, k:k + 1], degree_all[:, k:k + 1]).then_inc(s_deg_int, 1)

            def running_sum(buffers, ends):
                now, shift = 0, 1
                while shift < ends:
                    src, dst = buffers[now], buffers[1 - now]
                    nc.gpsimd.tensor_tensor(dst[..., shift:], src[..., shift:], src[..., :ends - shift], ALU.add)
                    nc.gpsimd.tensor_copy(dst[..., :shift], src[..., :shift])
                    pool.drain()
                    now, shift = 1 - now, 2 * shift
                return now

            def cap(b, t):
                u, k = TILES * b + t, t % MASKS
                wait_alone(pool, s_masked, u - FIRST + 1)
                largest_degree(u, k)
                wait_alone(pool, s_deg_int, u + 1)
                largest = load_numbers(nc.gpsimd, degree_int[0:1, k:k + 1], 0, N)
                with pool.If(largest[0] > SAMPLES):
                    nc.gpsimd.tensor_copy(in_group[:, 0, :, :], mask[:, k, :].rearrange("p (g i) -> p g i", i=GROUP))
                    pool.drain()
                    a = running_sum([in_group[:, j, :, :] for j in range(2)], GROUP)
                    nc.gpsimd.memset(of_groups[:, 0, 0:1], 0.0)
                    nc.gpsimd.tensor_copy(of_groups[:, 0, 1:], in_group[:, a, :N // GROUP - 1, GROUP - 1])
                    pool.drain()
                    g = running_sum([of_groups[:, j, :] for j in range(2)], N // GROUP)
                    nc.gpsimd.tensor_tensor(position[:, :, :], in_group[:, a, :, :],
                                            of_groups[:, g, :].unsqueeze(2).to_broadcast([P, N // GROUP, GROUP]), ALU.add)
                    pool.drain()
                    nc.gpsimd.tensor_scalar(kept[:, :], position[:, :, :].rearrange("p g i -> p (g i)"),
                                            float(SAMPLES) + 0.5, None, ALU.is_lt)
                    pool.drain()
                    nc.gpsimd.tensor_tensor(mask[:, k, :], mask[:, k, :], kept[:, :], ALU.mult)
                pool.drain().then_inc(s_capped, 1)

            def levels(b, par):
                wait_alone(pool, s_cmax, b + 1)
                nc.gpsimd.partition_all_reduce(count_all[:, par, :], count_max[:, par, :], P, all_max
                                               ).then_inc(s_call, 1)
                wait_alone(pool, s_call, b + 1)
                nc.gpsimd.tensor_copy(levels_int[:, par, :], count_all[:, par, :]).then_inc(s_levels, 1)

            def deviation(b):
                wait_alone(pool, s_sq, b + 1)
                nc.gpsimd.tensor_scalar(var_eps[:, :], sq_sum[:, :], 1.0 / C, EPS, ALU.mult, ALU.add
                                        ).then_inc(s_var, 1)
                wait_alone(pool, s_var, b + 1)
                nc.gpsimd.tensor_tensor(rstd[:, :], var_eps[:, :], half[:, :], ALU.pow).then_inc(s_rstd, 1)

            def add_skip(b, par, rnd):
                wait_alone(pool, s_relu, TILES * b + TILES)
                wait_alone(pool, s_skip[par], 16 * (rnd + 1))
                nc.gpsimd.tensor_tensor(y[:, par, :, :], relu[:, :, :], x_skip[:, par, :, :], ALU.add
                                        ).then_inc(s_y, 1)

            for u in range(FIRST):
                pool.wait_ge(s_first_masked, u + 1)
                largest_degree(u, u % MASKS)
                if u == 0:
                    deviation(0)
            levels(0, 0)

            def graph(b, par, rnd, pair):
                first, last = is_first(b), is_last(b)
                for t in range(TILES):
                    if t == TILES - 1 and not first:
                        before = rnd - 1 + par
                        if pair is None:
                            pool.wait_ge(s_stored[1 - par], 16 * before)
                        else:
                            with where(pool, pair > 0):
                                wait_alone(pool, s_stored[1 - par], 16 * before)
                        add_skip(b - 1, 1 - par, before)
                    if last:
                        continue
                    if t == 4:
                        split_lo(nc.gpsimd, pool, b + 1, 1 - par)
                    for ahead in masks_made(first, t):
                        with where(pool, tile_exists(par, pair, b, ahead)):
                            cap(b + 1 + ahead // TILES, ahead % TILES)
                    if t == 2:
                        deviation(b + 1)
                        normalise(nc.gpsimd, pool, b + 1, 1 - par)
                    elif t == 3:
                        split_rest(nc.gpsimd, pool, b + 1, 1 - par)
                    elif t == 7:
                        levels(b + 1, 1 - par)

            over_graphs(pool, graph)

        @block.vector
        def _(dve):
            level = dve.alloc_register("levels_folded")
            dve.reg_mov(level, 0)

            def first_mask(u):
                a, k = u % SLOTS, u % MASKS
                dve.wait_ge(s_adj[a], 16 * (u // SLOTS + 1))
                if u >= MASKS:
                    dve.wait_ge(s_transposed, u - MASKS + 1)
                nc.vector.tensor_scalar(mask[:, k, :], adj_in[:, a, :], 0.0, None, ALU.not_equal, ALU.add,
                                        accum_out=degree[:, k:k + 1]).then_inc(s_first_masked, 1)

            def first_cap(u):
                k = u % MASKS
                dve.wait_ge(s_deg_int, u + 1)
                largest = load_numbers(nc.vector, degree_int[0:1, k:k + 1], 0, N)
                with dve.If(largest[0] > SAMPLES):
                    nc.vector.tensor_tensor_scan(prefix[:, :], ones[:, :], mask[:, k, :], 0.0, ALU.mult, ALU.add)
                    dve.drain()
                    nc.vector.scalar_tensor_tensor(mask[:, k, :], prefix[:, :], float(SAMPLES), mask[:, k, :],
                                                   ALU.is_le, ALU.mult)
                dve.drain().then_inc(s_capped, 1)

            def split_bias():
                dve.wait_ge(s_bias, 16 * len(BIAS_ROWS))
                nc.vector.tensor_copy(bias_hi[:, :], bias_rows[:, :])
                dve.drain()
                nc.vector.tensor_tensor(bias_rest[:, :], bias_rows[:, :], bias_hi[:, :], ALU.subtract)
                dve.drain()
                nc.vector.tensor_copy(bias_mid[:, :], bias_rest[:, :])
                dve.drain()
                nc.vector.tensor_tensor(bias_lo[:, :], bias_rest[:, :], bias_mid[:, :], ALU.subtract)
                dve.drain()
                for row, part in zip(BIAS_ROWS, (bias_hi, bias_mid, bias_lo)):
                    last = nc.vector.tensor_copy(bias_parts[row:row + 1, :], part[row:row + 1, :])
                last.then_inc(s_bias_parts, 1)

            def make_onehot(par, t, k, buf):
                key = MARK + k if type(k) is int else level_val[:, bass.ds(k, 1)]
                nc.vector.tensor_scalar(onehot[:, bass.ds(buf, 1), :, :].rearrange("p a q n -> p (a q n)"),
                                        rank[:, par, t, :], key, None, ALU.is_equal).then_inc(s_onehot, 1)

            def tile_agg(par, t):
                return agg[:, par, P * t:P * (t + 1)]

            def level_top_of(k):
                return level_top[:, bass.ds(k, 1), :].rearrange("p a n -> p (a n)")

            def step(par, t, ahead, first=False, fold=None):
                now = dve.snap(level)
                buf = dve.snap(now % RING)
                top = dve.snap(now % TOPS)
                before = dve.snap((now + TOPS - 1) % TOPS)
                dve.wait_ge(s_gathered, now + 1)
                nc.vector.tensor_reduce(tile_agg(par, t) if first else level_top_of(top),
                                        gathered[:, bass.ds(buf, 1), :, :].rearrange("p a q n -> p (a n) q"),
                                        AX.X, ALU.max)
                if fold is not None:
                    if ahead is None:
                        dve.drain()
                    else:
                        dve.wait_ge(s_onehot, now + RING)
                    folded = nc.vector.tensor_tensor(tile_agg(*fold), tile_agg(*fold), level_top_of(before), ALU.max)
                    if fold[0] != par:
                        folded.then_inc(s_agg, 1)
                if ahead is not None:
                    make_onehot(*ahead, buf)
                dve.reg_add(level, level, 1)

            def count_maxima(b, par):
                dve.wait_ge(s_counts_sb, TILES * b + TILES)
                nc.vector.tensor_reduce(count_max[:, par, :], counts[:, par, :, :], AX.X, ALU.max).then_inc(s_cmax, 1)

            dve.wait_ge(s_consts, N_CONSTS)
            for u in range(FIRST + 1):
                if u < FIRST:
                    first_mask(u)
                if u == 4:
                    normalise(nc.vector, dve, 0, 0)
                elif u == 5:
                    split_rest(nc.vector, dve, 0, 0)
                elif u == 6:
                    split_bias()
                elif u == 7:
                    split_lo(nc.vector, dve, 0, 0)
                if u:
                    first_cap(u - 1)
            dve.wait_ge(s_rank_sb, 2)
            for k in range(RING):
                make_onehot(0, 0, k, k)
            count_maxima(0, 0)

            def graph(b, par, rnd, pair):
                first, last = is_first(b), is_last(b)
                n_levels = []
                for t in range(TILES):
                    if t < TILES - 1:
                        after = [(par, t + 1, k) for k in range(RING)]
                    elif last:
                        after = [None] * RING
                    else:
                        wait_alone(dve, s_rank_sb, 2 * (TILES * (b + 1) + 1))
                        after = [(1 - par, 0, k) for k in range(RING)]
                    here = (par, t)
                    before = (par, t - 1) if t else None if first else (1 - par, TILES - 1)
                    step(par, t, (par, t, RING), first=True, fold=before)
                    if t == 0:
                        wait_alone(dve, s_rank_sb, 2 * TILES * (b + 1))
                        wait_alone(dve, s_levels, b + 1)
                        n_levels = list(load_numbers(nc.vector, levels_int[0:1, par, :], MIN_LEVELS, SAMPLES))
                        lacking = dve.snap((2 * sum(n_levels[1:], n_levels[0])) % RING)
                        n_levels[-1] = dve.snap(n_levels[-1] + lacking)
                    with dve.If(n_levels[t] > MIN_LEVELS):
                        step(par, t, (par, t, MIN_LEVELS))
                        with dve.If(n_levels[t] > MIN_LEVELS + 1):
                            with dve.Fori(MIN_LEVELS + 1, n_levels[t]) as k:
                                step(par, t, (par, t, k), fold=here)
                        step(par, t, after[0], fold=here)
                    with dve.Else():
                        step(par, t, after[0])
                    step(par, t, after[1], fold=here)
                    if t == TILES - 1 and not last:
                        count_maxima(b + 1, 1 - par)
                    step(par, t, after[2], fold=here)

            over_graphs(dve, graph)
            dve.drain()
            final = tile_agg(1, TILES - 1)
            top = dve.snap((dve.snap(level) + (TOPS - 1)) % TOPS)
            nc.vector.tensor_tensor(final, final, level_top_of(top), ALU.max).then_inc(s_agg, 1)
            dve.wait_ge(s_stored[1], 16 * (NBATCH // 2 - 1))
            dve.wait_ge(s_skip[1], 16 * (NBATCH // 2))
            for s in range(TILES):
                dve.wait_ge(s_proj, TILES * LAST + s + 1)
                nc.vector.scalar_tensor_tensor(y[:, 1, s, :], last_projection(s), 0.0, x_skip[:, 1, s, :],
                                               ALU.max, ALU.add).then_inc(s_last_y, 1)

        @block.tensor
        def _(pe):
            level = pe.alloc_register("levels_gathered")
            pe.reg_mov(level, 0)

            def transpose_tile(u, t):
                pe.wait_ge(s_capped, u + 1)
                for q in range(Q):
                    last = nc.tensor.transpose(mask_tp[:, q, :], mask[:, t % MASKS, q:N:Q], ident_b[:, :])
                last.then_inc(s_transposed, 1)

            def rank_half(t, g, to):
                nc.tensor.matmul(to, rank_w[:, :], mask_t[:, t % 2, g * HALF:(g + 1) * HALF, :],
                                 start=True, stop=True).then_inc(s_ranked, 1)

            def count_tile(t, to):
                for q in range(Q):
                    last = nc.tensor.matmul(to[:, q:q + 1], mask_t[:, t % 2, q, :], ones[:, 0:1],
                                            start=True, stop=True)
                last.then_inc(s_counted, 1)

            def transpose_h(par, t):
                for k in range(H_PIECE):
                    last = nc.tensor.transpose(bank_b[:, k * P:(k + 1) * P], h[:, par, t * H_PIECE + k, :],
                                               ident_f[:, :])
                last.then_inc(s_h_tp, 1)

            def project(par, s, to):
                nc.tensor.matmul(to, ones[:, 0:P], bias_parts[:, :], start=True, stop=False)
                nc.tensor.matmul(to, h_t[:, par, s, :], w_sb[:, 0, :], start=False, stop=False)
                nc.tensor.matmul(to, agg[:, par, s:N:Q], w_sb[:, 1, :], start=False, stop=True).then_inc(s_proj, 1)

            def gather_level(par, buf, now):
                pe.wait_ge(s_onehot, now + buf + 1)
                for q in range(Q):
                    for part in range(PARTS):
                        last = nc.tensor.matmul(gathered[:, buf, q, :], h_parts[:, par, part, q, :],
                                                onehot[:, buf, q, :], start=(part == 0), stop=(part == PARTS - 1))
                last.then_inc(s_gathered, 1)

            pe.wait_ge(s_consts, N_CONSTS)
            for t in range(TILES + 1):
                if t >= 1:
                    pe.wait_ge(s_mask_t, t)
                if t < TILES:
                    transpose_tile(t, t)
                if t >= 1:
                    if t > RING:
                        pe.wait_ge(s_rank_sb, 2 * (t - RING))
                    for g in range(2):
                        rank_half(t - 1, g, gathered[:, (t - 1) % RING, g * HALF:(g + 1) * HALF, :])
                    if t >= 2:
                        pe.wait_ge(s_counts_sb, t - 1)
                    count_tile(t - 1, first_counts_ps)
            pe.wait_ge(s_weights, 16)
            pe.wait_ge(s_bias_parts, 1)
            pe.wait_ge(s_rank_sb, 2 * TILES)

            def graph(b, par, rnd, pair):
                first, last = is_first(b), is_last(b)
                pe.wait_ge(s_lo, b + 1)
                for t in range(TILES):
                    u = TILES * (b + 1) + t
                    now = pe.snap(level)
                    gather_level(par, 0, now)
                    if not last:
                        pe.wait_ge(s_counts_sb, u)
                        transpose_tile(u, t)
                    if t < H_PIECES:
                        if first and t == 0:
                            pe.wait_ge(s_counts_sb, TILES)
                        elif last and t > 0:
                            pe.wait_ge(s_h_t, H_PIECES * b + t)
                        else:
                            pe.wait_ge(s_rank_sb, 2 * u)
                        transpose_h(par, t)
                    gather_level(par, 1, now)
                    if not last:
                        pe.wait_ge(s_mask_t, u + 1)
                        if t < H_PIECES:
                            pe.wait_ge(s_h_t, H_PIECES * b + t + 1)
                        else:
                            pe.wait_ge(s_rank_sb, 2 * u)
                        rank_half(t, 0, bank_b[:, :])
                    gather_level(par, 2, now)
                    if not last:
                        pe.wait_ge(s_rank_sb, 2 * u + 1)
                        rank_half(t, 1, bank_b[:, :])
                        count_tile(t, counts_ps)
                    if not first:
                        if t == 0:
                            pe.wait_ge(s_agg, b)
                            pe.wait_ge(s_h_t, H_PIECES * b)
                        if last:
                            if t == 0:
                                pe.wait_ge(s_counts_sb, u)
                            else:
                                pe.wait_ge(s_relu, TILES * (b - 1) + t)
                        project(1 - par, t, projection)
                    pe.reg_add(level, level, RING)
                    if t == 0:
                        wait_alone(pe, s_levels, b + 1)
                        n_levels = load_numbers(nc.tensor, levels_int[0:1, par, :], MIN_LEVELS, SAMPLES)
                        rounds = pe.snap((sum(n_levels[1:], n_levels[0]) + (RING - 1)) // RING - TILES)
                    begin = pe.snap(rounds * t // TILES)
                    end = pe.snap(rounds * (t + 1) // TILES)
                    with pe.If(begin < end):
                        with pe.Fori(begin, end):
                            now = pe.snap(level)
                            for buf in range(RING):
                                gather_level(par, buf, now)
                            pe.reg_add(level, level, RING)

            over_graphs(pe, graph)
            pe.wait_ge(s_agg, NBATCH)
            pe.wait_ge(s_h_t, H_PIECES * NBATCH)
            pe.wait_ge(s_relu, TILES * LAST)
            for s in range(TILES):
                project(1, s, last_projection(s))


def kernel(x, adj, L0_gnn_W, L0_gnn_b):
    import numpy as np
    import concourse.bacc as bacc
    from concourse import mybir
    from concourse.bass_utils import run_bass_kernel_spmd

    nc = bacc.Bacc("TRN2", target_bir_lowering=False, num_devices=1)
    arrays, args = {}, []
    for name, a in (("x", x), ("adj", adj), ("w", L0_gnn_W), ("bias", L0_gnn_b)):
        a = np.ascontiguousarray(a)
        arrays[name] = a
        args.append(nc.dram_tensor(name, a.shape, mybir.dt.from_np(a.dtype), kind="ExternalInput").ap())
    args.append(nc.dram_tensor("out", arrays["x"].shape, mybir.dt.float32, kind="ExternalOutput").ap())
    gnn_layer(nc, *args)
    result = run_bass_kernel_spmd(nc, [arrays], core_ids=[0])
    return result.results[0]["out"]
```

```python
from contextlib import ExitStack, nullcontext

import concourse.bass as bass
from concourse import mybir

F32 = mybir.dt.float32
BF16 = mybir.dt.bfloat16
I32 = mybir.dt.int32
ALU = mybir.AluOpType
ACT = mybir.ActivationFunctionType
AX = mybir.AxisListType


def gnn_layer(nc, x, adj, w, bias, out):
    P = 128
    NBATCH, N, C = x.shape
    OUT = w.shape[1]
    Q = N // P
    TILES = N // P
    ALL_TILES = NBATCH * TILES
    SAMPLES = 25
    EPS = 1e-5
    PARTS = 3
    MARK = 128.0
    RING = 3
    MIN_LEVELS = RING + 1
    TOPS = 4
    KVALS = 32
    SLOTS = 4
    MASKS = 8
    LEAD = 4
    FIRST = TILES + LEAD
    GROUP = 8
    HALF = Q // 2
    H_PIECES = 4
    H_PIECE = Q // H_PIECES
    MIDDLE = (NBATCH - 2) // 2
    LAST = NBATCH - 1
    BIAS_ROWS = (0, 32, 64)
    N_CONSTS = 13

    x_v = x.rearrange("b (p q) c -> b p (q c)", q=Q)
    out_v = out.rearrange("b (p q) c -> b p (q c)", q=Q)
    adj_v = adj.rearrange("b (t p) j -> b t p j", p=P)

    ctx = ExitStack()
    with ctx:
        def sb(name, shape, dt):
            return ctx.enter_context(nc.sbuf_tensor(name, shape, dt))

        def ps(name, shape, dt):
            return ctx.enter_context(nc.psum_tensor(name, shape, dt))

        def sem(name):
            return ctx.enter_context(nc.semaphore(name))

        ident_b = sb("ident_b", [P, P], BF16)
        ident_f = sb("ident_f", [P, P], F32)
        rank_w = sb("rank_w", [P, P], BF16)
        ones = sb("ones", [P, N], BF16)
        level_val = sb("level_val", [P, KVALS], F32)
        half = sb("half", [P, Q], F32)
        w_sb = sb("w_sb", [P, 2, OUT], F32)
        bias_rows = sb("bias_rows", [P, OUT], F32)
        bias_hi = sb("bias_hi", [P, OUT], BF16)
        bias_rest = sb("bias_rest", [P, OUT], F32)
        bias_mid = sb("bias_mid", [P, OUT], BF16)
        bias_lo = sb("bias_lo", [P, OUT], BF16)
        bias_parts = sb("bias_parts", [P, OUT], BF16)
        adj_in = sb("adj_in", [P, SLOTS, N], I32)
        sign = sb("sign", [P, 2, N], BF16)
        mask = sb("mask", [P, MASKS, N], BF16)
        degree = sb("degree", [P, MASKS], F32)
        degree_all = sb("degree_all", [P, MASKS], F32)
        degree_int = sb("degree_int", [P, MASKS], I32)
        in_group = sb("in_group", [P, N // GROUP, GROUP], F32)
        in_group2 = sb("in_group2", [P, N // GROUP ** 2, GROUP], F32)
        in_group3 = sb("in_group3", [P, N // GROUP ** 3, GROUP], F32)
        before3_t = sb("before3", [P, N // GROUP ** 3], F32)
        before2_t = sb("before2", [P, N // GROUP ** 3, GROUP], F32)
        before1_t = sb("before1", [P, N // GROUP ** 2, GROUP], F32)
        before3, before2, before1 = before3_t[:, :], before2_t[:, :, :], before1_t[:, :, :]
        position = sb("position", [P, N // GROUP, GROUP], F32)
        kept = sb("kept", [P, N], BF16)
        prefix = sb("prefix", [P, N], BF16)
        mask_t = sb("mask_t", [P, 2, Q, P], BF16)
        rank = sb("rank", [P, 2, TILES, Q * P], BF16)
        counts = sb("counts", [P, 2, TILES, Q + 1], F32)
        count_max = sb("count_max", [P, 2, TILES], F32)
        count_all = sb("count_all", [P, 2, TILES], F32)
        levels_int = sb("levels_int", [P, 2, TILES], I32)
        x_in = sb("x_in", [P, 2, Q, C], F32)
        x_skip = sb("x_skip", [P, 2, Q, C], F32)
        trash = sb("trash", [P, Q, C], BF16)
        neg_mean = sb("neg_mean", [P, Q], F32)
        sq_sum = sb("sq_sum", [P, Q], F32)
        var_eps = sb("var_eps", [P, Q], F32)
        rstd = sb("rstd", [P, Q], F32)
        h_norm = sb("h_norm", [P, Q, C], F32)
        h = sb("h", [P, 2, Q, C], F32)
        h_parts = sb("h_parts", [P, 2, PARTS, Q, C], BF16)
        h_rest = sb("h_rest", [P, Q, C], F32)
        h_t = sb("h_t", [P, 2, Q, P], F32)
        onehot = sb("onehot", [P, RING, Q, P], BF16)
        level_top = sb("level_top", [P, TOPS, P], F32)
        agg = sb("agg", [P, 2, N], F32)
        relu = sb("relu", [P, Q, OUT], F32)
        y = sb("y", [P, 2, Q, OUT], F32)

        gathered = ps("gathered", [P, RING, Q, P], F32)
        bank_a = ps("bank_a", [P, 512], F32)
        bank_b = ps("bank_b", [P, 512], F32)
        mask_tp = bank_a[:, :].bitcast(BF16).rearrange("p (q n) -> p q n", q=Q)
        projection = bank_a[:, 0:OUT]
        counts_ps = bank_a[:, OUT:OUT + Q]
        first_counts_ps = bank_b[:, 0:Q]

        s_passed = {e: sem("passed_" + e) for e in ("SP", "Activation", "Pool", "DVE", "PE")}
        s_consts = sem("consts")
        s_weights = sem("weights")
        s_bias = sem("bias_loaded")
        s_bias_parts = sem("bias_parts_done")
        s_x = [sem(f"x_loaded{k}") for k in range(2)]
        s_skip = [sem(f"x_skip_loaded{k}") for k in range(2)]
        s_adj = [sem(f"adj_loaded{k}") for k in range(SLOTS)]
        s_stored = [sem(f"stored{k}") for k in range(2)]
        s_first_masked = sem("first_masked")
        s_signed = sem("signed")
        s_masked = sem("masked")
        s_deg_all = sem("degree_all_done")
        s_deg_int = sem("degree_int_done")
        s_capped = sem("capped")
        s_transposed = sem("mask_transposed")
        s_mask_t = sem("mask_t_copied")
        s_ranked = sem("ranked")
        s_rank_sb = sem("rank_copied")
        s_counted = sem("counted")
        s_counts_sb = sem("counts_copied")
        s_cmax = sem("count_max_done")
        s_call = sem("count_all_done")
        s_levels = sem("levels_known")
        s_mean = sem("neg_mean_done")
        s_sq = sem("sq_sum_done")
        s_var = sem("var_done")
        s_rstd = sem("rstd_done")
        s_norm = sem("h_norm_done")
        s_h = sem("h_done")
        s_hi = sem("h_hi_done")
        s_rest = sem("h_rest_done")
        s_mid = sem("h_mid_done")
        s_lo = sem("h_lo_done")
        s_h_tp = sem("h_transposed")
        s_h_t = sem("h_t_copied")
        s_onehot = sem("onehot_ready")
        s_gathered = sem("level_gathered")
        s_agg = sem("agg_ready")
        s_proj = sem("projected")
        s_relu = sem("relu_done")
        s_y = sem("y_ready")
        s_last_y = sem("last_y_ready")

        block = ctx.enter_context(nc.Block())

        def over_graphs(eng, graph):
            graph(0, 0, 0, None)
            with eng.Fori(0, MIDDLE) as pair:
                graph(2 * pair + 1, 1, pair, pair)
                graph(2 * pair + 2, 0, pair + 1, pair)
            graph(LAST, 1, LAST // 2, None)

        def where(eng, cond):
            return nullcontext() if cond is True else eng.If(cond)

        def earlier(n):
            return n if type(n) is int else n & 0xFFFF

        def wait_alone(eng, semaphore, value):
            eng.wait_ge(semaphore, value)
            if type(value) is not int:
                eng.sem_inc(s_passed[eng.engine.name], 1)

        def is_first(b):
            return type(b) is int and b == 0

        def is_last(b):
            return type(b) is int and b == LAST

        def tile_exists(par, pair, b, t):
            if t < TILES or pair is None:
                return True
            return True if par == 1 else pair < MIDDLE - 1

        @block.sync
        def _(sp):
            def existing(b):
                return b if type(b) is int else nc.s_assert_within(
                    b, 0, NBATCH - 1, skip_runtime_bounds_check_because="the loop's branches bound it")

            def load_x(b, par):
                sp.dma_start(x_in[:, par, :, :].rearrange("p q c -> p (q c)"),
                             x_v[existing(b)]).then_inc(s_x[par], 16)

            def load_tile(b, t):
                sp.dma_start(adj_in[:, t % SLOTS, :], adj_v[existing(b), t]).then_inc(s_adj[t % SLOTS], 16)

            def store(b, par):
                sp.dma_start(out_v[existing(b)], y[:, par, :, :].rearrange("p q c -> p (q c)")
                             ).then_inc(s_stored[par], 16)

            load_x(0, 0)
            for t in range(SLOTS):
                load_tile(0, t)
            sp.dma_start(w_sb[:, :, :], w.rearrange("(g p) o -> p g o", p=P)).then_inc(s_weights, 16)
            sp.wait_ge(s_consts, N_CONSTS)
            for row in BIAS_ROWS:
                sp.dma_start(bias_rows[row:row + 1, :], bias.rearrange("(a o) -> a o", a=1)).then_inc(s_bias, 16)
            for u in range(SLOTS, FIRST + SLOTS):
                sp.wait_ge(s_first_masked, u - SLOTS + 1)
                load_tile(u // TILES, u % TILES)
                if u == TILES - 1:
                    load_x(1, 1)

            def graph(b, par, rnd, pair):
                if not is_first(b):
                    with where(sp, True if par == 0 or pair is None else pair > 0):
                        wait_alone(sp, s_y, b - 1)
                        store(b - 2, par)
                sp.dma_start(x_skip[:, par, :, :].rearrange("p q c -> p (q c)"),
                             x_v[b]).then_inc(s_skip[par], 16)
                if not is_last(b):
                    with where(sp, tile_exists(par, pair, b, TILES)):
                        wait_alone(sp, s_norm, b + 1)
                        load_x(b + 2, par)
                    for t in range(LEAD + SLOTS, LEAD + SLOTS + TILES):
                        with where(sp, tile_exists(par, pair, b, t)):
                            wait_alone(sp, s_signed, TILES * (b + 1) + t - SLOTS - FIRST + 1)
                            load_tile(b + 1 + t // TILES, t % TILES)

            over_graphs(sp, graph)
            sp.wait_ge(s_y, LAST)
            store(LAST - 1, 0)
            for g in range(2):
                sp.wait_ge(s_last_y, HALF * (g + 1))
                sp.dma_start(out_v[LAST, :, g * HALF * C:(g + 1) * HALF * C],
                             y[:, 1, g * HALF:(g + 1) * HALF, :].rearrange("p q c -> p (q c)")
                             ).then_inc(s_stored[1], 16)
            sp.wait_ge(s_stored[0], 16 * (NBATCH // 2))
            sp.wait_ge(s_stored[1], 16 * (NBATCH // 2 + 1))

        @block.scalar
        def _(act):
            def sign_tile(t, rounds):
                act.wait_ge(s_adj[t % SLOTS], 16 * (rounds + 1))
                nc.scalar.activation(sign[:, t % 2, :], adj_in[:, t % SLOTS, :], ACT.Sign).then_inc(s_signed, 1)

            def square_tile(b, t):
                act.wait_ge(s_signed, TILES * b + t - FIRST + 1)
                nc.scalar.activation(mask[:, t % MASKS, :], sign[:, t % 2, :], ACT.Square,
                                     accum_out=degree[:, t:t + 1]).then_inc(s_masked, 1)

            def mask_t_copy(u, t):
                act.wait_ge(s_transposed, u + 1)
                nc.scalar.activation(mask_t[:, t % 2, :, :], mask_tp, ACT.Copy).then_inc(s_mask_t, 1)

            def rank_copy(u, par, t, g):
                act.wait_ge(s_ranked, 2 * u + g + 1)
                nc.scalar.activation(rank[:, par, t, g * HALF * P:(g + 1) * HALF * P], bank_b[:, :],
                                     ACT.Copy).then_inc(s_rank_sb, 1)

            def counts_copy(u, par, t, source):
                act.wait_ge(s_counted, u + 1)
                nc.scalar.activation(counts[:, par, t, 0:Q], source, ACT.Copy).then_inc(s_counts_sb, 1)

            def means(b, par, rnd, blocks):
                act.wait_ge(s_x[par], 16 * (rnd + 1))
                for q in blocks:
                    last = nc.scalar.activation(trash[:, q, :], x_in[:, par, q, :], ACT.Copy, scale=-1.0 / C,
                                                accum_out=neg_mean[:, q:q + 1])
                if Q - 1 in blocks:
                    last.then_inc(s_mean, 1)

            def squares(b, par, blocks):
                act.wait_ge(s_mean, b + 1)
                for q in blocks:
                    last = nc.scalar.activation(trash[:, q, :], x_in[:, par, q, :], ACT.Square,
                                                bias=neg_mean[:, q:q + 1], accum_out=sq_sum[:, q:q + 1])
                if Q - 1 in blocks:
                    last.then_inc(s_sq, 1)

            def h_relu(b, par):
                act.wait_ge(s_norm, b + 1)
                nc.scalar.activation(h[:, par, :, :], h_norm[:, :, :], ACT.Relu).then_inc(s_h, 1)

            def h_hi(b, par):
                act.wait_ge(s_h, b + 1)
                nc.scalar.activation(h_parts[:, par, 0, :, :], h[:, par, :, :], ACT.Copy).then_inc(s_hi, 1)

            def h_mid(b, par):
                act.wait_ge(s_rest, b + 1)
                nc.scalar.activation(h_parts[:, par, 1, :, :], h_rest[:, :, :], ACT.Copy).then_inc(s_mid, 1)

            def h_t_copy(b, par, t):
                act.wait_ge(s_h_tp, H_PIECES * b + t + 1)
                nc.scalar.activation(h_t[:, par, t * H_PIECE:(t + 1) * H_PIECE, :],
                                     bank_b[:, 0:H_PIECE * P], ACT.Copy).then_inc(s_h_t, 1)

            def relu_copy(b, s):
                act.wait_ge(s_proj, TILES * b + s + 1)
                nc.scalar.activation(relu[:, s, :], projection, ACT.Relu).then_inc(s_relu, 1)

            means(0, 0, 0, range(Q))
            squares(0, 0, range(Q))
            for t in range(TILES + 1):
                if t < TILES:
                    mask_t_copy(t, t)
                if t >= 1:
                    act.wait_ge(s_ranked, 2 * t)
                    nc.scalar.activation(rank[:, 0, t - 1, :],
                                         gathered[:, (t - 1) % RING, :, :].rearrange("p q n -> p (q n)"),
                                         ACT.Copy).then_inc(s_rank_sb, 2)
                    counts_copy(t - 1, 0, t - 1, first_counts_ps)
                if t == 3:
                    h_relu(0, 0)
                    h_hi(0, 0)
                elif t == 5:
                    h_mid(0, 0)
            def graph(b, par, rnd, pair):
                first, last = is_first(b), is_last(b)
                for t in range(TILES):
                    u = TILES * (b + 1) + t
                    ahead = t + LEAD
                    if t == 0 and not first:
                        rank_copy(u - 1, par, TILES - 1, 1)
                    elif t > 0 and not last:
                        rank_copy(u - 1, 1 - par, t - 1, 1)
                    if not last:
                        mask_t_copy(u, t)
                        with where(act, tile_exists(par, pair, b, ahead)):
                            sign_tile(ahead % TILES, TILES // SLOTS * (b + 1) + ahead // SLOTS)
                    if t < H_PIECES:
                        h_t_copy(b, par, t)
                    if not last:
                        if t < 2:
                            means(b + 1, 1 - par, rnd + par, range(4 * t, 4 * t + 2))
                        elif t < 4:
                            squares(b + 1, 1 - par, range(4 * t - 8, 4 * t - 6))
                        elif t == 5:
                            h_relu(b + 1, 1 - par)
                        elif t == 7:
                            h_mid(b + 1, 1 - par)
                        rank_copy(u, 1 - par, t, 0)
                    if not first:
                        if t == 0:
                            with where(act, True if par == 0 or pair is None else pair > 0):
                                wait_alone(act, s_y, b - 1)
                        relu_copy(b - 1, t)
                    if last:
                        continue
                    counts_copy(u, 1 - par, t, counts_ps)
                    with where(act, tile_exists(par, pair, b, ahead)):
                        square_tile(b + 1 + ahead // TILES, ahead % TILES)
                    if t < 2:
                        means(b + 1, 1 - par, rnd + par, range(4 * t + 2, 4 * t + 4))
                    elif t < 4:
                        squares(b + 1, 1 - par, range(4 * t - 6, 4 * t - 4))
                    elif t == 5:
                        h_hi(b + 1, 1 - par)

            over_graphs(act, graph)

        def normalise(api, eng, b, par):
            wait_alone(eng, s_rstd, b + 1)
            for q in range(Q):
                last = api.tensor_scalar(h_norm[:, q, :], x_in[:, par, q, :], neg_mean[:, q:q + 1],
                                         rstd[:, q:q + 1], ALU.add, ALU.mult)
            last.then_inc(s_norm, 1)

        def split_rest(api, eng, b, par):
            wait_alone(eng, s_hi, b + 1)
            api.tensor_tensor(h_rest[:, :, :], h[:, par, :, :], h_parts[:, par, 0, :, :],
                              ALU.subtract).then_inc(s_rest, 1)

        def split_lo(api, eng, b, par):
            wait_alone(eng, s_mid, b + 1)
            api.tensor_tensor(h_parts[:, par, 2, :, :], h_rest[:, :, :], h_parts[:, par, 1, :, :],
                              ALU.subtract).then_inc(s_lo, 1)

        def last_projection(s):
            if s < 2 * RING:
                return gathered[:, s // 2, HALF * (s % 2), :]
            return (bank_a, bank_b)[s - 2 * RING][:, 0:OUT]

        def load_numbers(engine, numbers, least, most):
            return nc.values_load_multi_w_load_instructions(
                numbers, engines=[engine.engine], min_val=least, max_val=most,
                skip_runtime_bounds_check_because="a row has at most N neighbours")[1]

        @block.gpsimd
        def _(pool):
            nc.gpsimd.memset(bias_rows[:, :], 0.0).then_inc(s_consts, 1)
            nc.gpsimd.memset(bias_parts[:, :], 0.0).then_inc(s_consts, 1)
            nc.gpsimd.memset(counts[:, :, :, :], float(MIN_LEVELS)).then_inc(s_consts, 1)
            nc.gpsimd.memset(ident_b[:, :], 0.0).then_inc(s_consts, 1)
            nc.gpsimd.memset(ident_f[:, :], 0.0).then_inc(s_consts, 1)
            nc.gpsimd.memset(rank_w[:, :], 1.0).then_inc(s_consts, 1)
            nc.gpsimd.memset(ones[:, :], 1.0).then_inc(s_consts, 1)
            nc.gpsimd.memset(half[:, :], -0.5).then_inc(s_consts, 1)
            nc.gpsimd.iota(level_val[:, :], pattern=[[1, KVALS]], base=int(MARK), channel_multiplier=0,
                           allow_small_or_imprecise_dtypes=True).then_inc(s_consts, 1)
            wait_alone(pool, s_consts, 9)
            for m in (ident_b, ident_f):
                nc.gpsimd.affine_select(out=m[:, :], in_=m[:, :], compare_op=ALU.not_equal, fill=1.0, base=0,
                                        pattern=[[-1, P]], channel_multiplier=1).then_inc(s_consts, 1)
            nc.gpsimd.affine_select(out=rank_w[:, :], in_=rank_w[:, :], compare_op=ALU.is_gt, fill=0.0, base=0,
                                    pattern=[[1, P]], channel_multiplier=-1).then_inc(s_consts, 1)
            wait_alone(pool, s_consts, 12)
            nc.gpsimd.affine_select(out=rank_w[:, :], in_=rank_w[:, :], compare_op=ALU.not_equal, fill=MARK,
                                    base=0, pattern=[[1, P]], channel_multiplier=-1).then_inc(s_consts, 1)
            all_max = bass.bass_isa.ReduceOp.max

            def largest_degree(u, k):
                nc.gpsimd.partition_all_reduce(degree_all[:, k:k + 1], degree[:, k:k + 1], P, all_max
                                               ).then_inc(s_deg_all, 1)
                wait_alone(pool, s_deg_all, u + 1)
                nc.gpsimd.tensor_copy(degree_int[:, k:k + 1], degree_all[:, k:k + 1]).then_inc(s_deg_int, 1)

            def group_sums(out, numbers):
                nc.gpsimd.tensor_copy(out[..., 0], numbers[..., 0])
                for i in range(1, GROUP):
                    pool.drain()
                    nc.gpsimd.tensor_tensor(out[..., i], out[..., i - 1], numbers[..., i], ALU.add)
                pool.drain()

            def shifted_by(out, start, sums):
                nc.gpsimd.tensor_copy(out[..., 0], start)
                nc.gpsimd.tensor_tensor(out[..., 1:], sums[..., :GROUP - 1],
                                        start.unsqueeze(2).to_broadcast([P, start.shape[1], GROUP - 1]), ALU.add)
                pool.drain()

            def cap(b, t):
                u, k = TILES * b + t, t % MASKS
                wait_alone(pool, s_masked, u - FIRST + 1)
                largest_degree(u, k)
                wait_alone(pool, s_deg_int, u + 1)
                largest = load_numbers(nc.gpsimd, degree_int[0:1, k:k + 1], 0, N)
                with pool.If(largest[0] > SAMPLES):
                    group_sums(in_group, mask[:, k, :].rearrange("p (g i) -> p g i", i=GROUP))
                    group_sums(in_group2, in_group[:, :, GROUP - 1].rearrange("p (g i) -> p g i", i=GROUP))
                    group_sums(in_group3, in_group2[:, :, GROUP - 1].rearrange("p (g i) -> p g i", i=GROUP))
                    nc.gpsimd.memset(before3[:, 0:1], 0.0)
                    nc.gpsimd.tensor_copy(before3[:, 1:2], in_group3[:, 0, GROUP - 1:GROUP])
                    pool.drain()
                    shifted_by(before2, before3, in_group3)
                    shifted_by(before1, before2.rearrange("p g i -> p (g i)"), in_group2)
                    nc.gpsimd.tensor_tensor(position[:, :, :], in_group[:, :, :],
                                            before1.rearrange("p g i -> p (g i)").unsqueeze(2).to_broadcast(
                                                [P, N // GROUP, GROUP]), ALU.add)
                    pool.drain()
                    nc.gpsimd.tensor_scalar(kept[:, :], position[:, :, :].rearrange("p g i -> p (g i)"),
                                            float(SAMPLES) + 0.5, None, ALU.is_lt)
                    pool.drain()
                    nc.gpsimd.tensor_tensor(mask[:, k, :], mask[:, k, :], kept[:, :], ALU.mult)
                pool.drain().then_inc(s_capped, 1)

            def levels(b, par):
                wait_alone(pool, s_cmax, b + 1)
                nc.gpsimd.partition_all_reduce(count_all[:, par, :], count_max[:, par, :], P, all_max
                                               ).then_inc(s_call, 1)
                wait_alone(pool, s_call, b + 1)
                nc.gpsimd.tensor_copy(levels_int[:, par, :], count_all[:, par, :]).then_inc(s_levels, 1)

            def deviation(b):
                wait_alone(pool, s_sq, b + 1)
                nc.gpsimd.tensor_scalar(var_eps[:, :], sq_sum[:, :], 1.0 / C, EPS, ALU.mult, ALU.add
                                        ).then_inc(s_var, 1)
                wait_alone(pool, s_var, b + 1)
                nc.gpsimd.tensor_tensor(rstd[:, :], var_eps[:, :], half[:, :], ALU.pow).then_inc(s_rstd, 1)

            def add_skip(b, par, rnd, stored):
                with where(pool, stored):
                    wait_alone(pool, s_stored[par], earlier(16 * rnd))
                wait_alone(pool, s_relu, TILES * b + TILES)
                wait_alone(pool, s_skip[par], 16 * (rnd + 1))
                nc.gpsimd.tensor_tensor(y[:, par, :, :], relu[:, :, :], x_skip[:, par, :, :], ALU.add
                                        ).then_inc(s_y, 1)

            for u in range(FIRST):
                pool.wait_ge(s_first_masked, u + 1)
                largest_degree(u, u % MASKS)
                if u == 0:
                    deviation(0)
            levels(0, 0)

            def graph(b, par, rnd, pair):
                first, last = is_first(b), is_last(b)
                for t in range(TILES):
                    if t == 0 and not first:
                        with where(pool, True if par == 0 or pair is None else pair > 0):
                            add_skip(b - 2, par, rnd - 1, True if pair is None else pair > par)
                    if last:
                        continue
                    if t == 5:
                        split_rest(nc.gpsimd, pool, b + 1, 1 - par)
                    elif t == 7:
                        split_lo(nc.gpsimd, pool, b + 1, 1 - par)
                        levels(b + 1, 1 - par)
                    ahead = t + LEAD
                    with where(pool, tile_exists(par, pair, b, ahead)):
                        cap(b + 1 + ahead // TILES, ahead % TILES)
                    if t == 3:
                        deviation(b + 1)
                        normalise(nc.gpsimd, pool, b + 1, 1 - par)

            over_graphs(pool, graph)
            add_skip(LAST - 1, 0, MIDDLE, True)

        @block.vector
        def _(dve):
            level = dve.alloc_register("levels_folded")
            dve.reg_mov(level, 0)

            def first_mask(u):
                a, k = u % SLOTS, u % MASKS
                dve.wait_ge(s_adj[a], 16 * (u // SLOTS + 1))
                if u >= MASKS:
                    dve.wait_ge(s_transposed, u - MASKS + 1)
                nc.vector.tensor_scalar(mask[:, k, :], adj_in[:, a, :], 0.0, None, ALU.not_equal, ALU.add,
                                        accum_out=degree[:, k:k + 1]).then_inc(s_first_masked, 1)

            def first_cap(u):
                k = u % MASKS
                dve.wait_ge(s_deg_int, u + 1)
                largest = load_numbers(nc.vector, degree_int[0:1, k:k + 1], 0, N)
                with dve.If(largest[0] > SAMPLES):
                    nc.vector.tensor_tensor_scan(prefix[:, :], ones[:, :], mask[:, k, :], 0.0, ALU.mult, ALU.add)
                    dve.drain()
                    nc.vector.scalar_tensor_tensor(mask[:, k, :], prefix[:, :], float(SAMPLES), mask[:, k, :],
                                                   ALU.is_le, ALU.mult)
                dve.drain().then_inc(s_capped, 1)

            def split_bias():
                dve.wait_ge(s_bias, 16 * len(BIAS_ROWS))
                nc.vector.tensor_copy(bias_hi[:, :], bias_rows[:, :])
                dve.drain()
                nc.vector.tensor_tensor(bias_rest[:, :], bias_rows[:, :], bias_hi[:, :], ALU.subtract)
                dve.drain()
                nc.vector.tensor_copy(bias_mid[:, :], bias_rest[:, :])
                dve.drain()
                nc.vector.tensor_tensor(bias_lo[:, :], bias_rest[:, :], bias_mid[:, :], ALU.subtract)
                dve.drain()
                for row, part in zip(BIAS_ROWS, (bias_hi, bias_mid, bias_lo)):
                    last = nc.vector.tensor_copy(bias_parts[row:row + 1, :], part[row:row + 1, :])
                last.then_inc(s_bias_parts, 1)

            def make_onehot(par, t, k, buf):
                key = MARK + k if type(k) is int else level_val[:, bass.ds(k, 1)]
                nc.vector.tensor_scalar(onehot[:, bass.ds(buf, 1), :, :].rearrange("p a q n -> p (a q n)"),
                                        rank[:, par, t, :], key, None, ALU.is_equal).then_inc(s_onehot, 1)

            def tile_agg(par, t):
                return agg[:, par, P * t:P * (t + 1)]

            def level_top_of(k):
                return level_top[:, bass.ds(k, 1), :].rearrange("p a n -> p (a n)")

            def step(par, t, ahead, first=False, fold=None):
                now = dve.snap(level)
                buf = dve.snap(now % RING)
                top = dve.snap(now % TOPS)
                before = dve.snap((now + TOPS - 1) % TOPS)
                dve.wait_ge(s_gathered, now + 1)
                nc.vector.tensor_reduce(tile_agg(par, t) if first else level_top_of(top),
                                        gathered[:, bass.ds(buf, 1), :, :].rearrange("p a q n -> p (a n) q"),
                                        AX.X, ALU.max)
                if fold is not None:
                    if ahead is None:
                        dve.drain()
                    else:
                        dve.wait_ge(s_onehot, now + RING)
                    folded = nc.vector.tensor_tensor(tile_agg(*fold), tile_agg(*fold), level_top_of(before), ALU.max)
                    if fold[0] != par:
                        folded.then_inc(s_agg, 1)
                if ahead is not None:
                    make_onehot(*ahead, buf)
                dve.reg_add(level, level, 1)

            def count_maxima(b, par):
                dve.wait_ge(s_counts_sb, TILES * b + TILES)
                nc.vector.tensor_reduce(count_max[:, par, :], counts[:, par, :, :], AX.X, ALU.max).then_inc(s_cmax, 1)

            dve.wait_ge(s_consts, N_CONSTS)
            for u in range(FIRST + 1):
                if u < FIRST:
                    first_mask(u)
                if u == 4:
                    normalise(nc.vector, dve, 0, 0)
                elif u == 6:
                    split_rest(nc.vector, dve, 0, 0)
                elif u == 8:
                    split_lo(nc.vector, dve, 0, 0)
                elif u == 9:
                    dve.wait_ge(s_rank_sb, 2)
                    for k in range(RING):
                        make_onehot(0, 0, k, k)
                if u:
                    first_cap(u - 1)
            count_maxima(0, 0)
            split_bias()

            def graph(b, par, rnd, pair):
                first, last = is_first(b), is_last(b)
                n_levels = []
                for t in range(TILES):
                    if t < TILES - 1:
                        after = [(par, t + 1, k) for k in range(RING)]
                    elif last:
                        after = [None] * RING
                    else:
                        wait_alone(dve, s_rank_sb, 2 * (TILES * (b + 1) + 1))
                        after = [(1 - par, 0, k) for k in range(RING)]
                    here = (par, t)
                    before = (par, t - 1) if t else None if first else (1 - par, TILES - 1)
                    step(par, t, (par, t, RING), first=True, fold=before)
                    if t == 1:
                        wait_alone(dve, s_rank_sb, 2 * TILES * (b + 1))
                    if t == 0:
                        wait_alone(dve, s_rank_sb, 2 * TILES * (b + 1) - 1)
                        wait_alone(dve, s_levels, b + 1)
                        n_levels = list(load_numbers(nc.vector, levels_int[0:1, par, :], MIN_LEVELS, SAMPLES))
                        lacking = dve.snap((2 * sum(n_levels[1:], n_levels[0])) % RING)
                        n_levels[-1] = dve.snap(n_levels[-1] + lacking)
                    with dve.If(n_levels[t] > MIN_LEVELS):
                        step(par, t, (par, t, MIN_LEVELS))
                        with dve.If(n_levels[t] > MIN_LEVELS + 1):
                            with dve.Fori(MIN_LEVELS + 1, n_levels[t]) as k:
                                step(par, t, (par, t, k), fold=here)
                        step(par, t, after[0], fold=here)
                    with dve.Else():
                        step(par, t, after[0])
                    step(par, t, after[1], fold=here)
                    if t == TILES - 1 and not last:
                        count_maxima(b + 1, 1 - par)
                    step(par, t, after[2], fold=here)

            over_graphs(dve, graph)
            dve.drain()
            final = tile_agg(1, TILES - 1)
            top = dve.snap((dve.snap(level) + (TOPS - 1)) % TOPS)
            nc.vector.tensor_tensor(final, final, level_top_of(top), ALU.max).then_inc(s_agg, 1)
            dve.wait_ge(s_stored[1], 16 * (NBATCH // 2 - 1))
            dve.wait_ge(s_skip[1], 16 * (NBATCH // 2))
            for s in range(TILES):
                dve.wait_ge(s_proj, TILES * LAST + s + 1)
                nc.vector.scalar_tensor_tensor(y[:, 1, s, :], last_projection(s), 0.0, x_skip[:, 1, s, :],
                                               ALU.max, ALU.add).then_inc(s_last_y, 1)

        @block.tensor
        def _(pe):
            level = pe.alloc_register("levels_gathered")
            pe.reg_mov(level, 0)

            def transpose_tile(u, t):
                pe.wait_ge(s_capped, u + 1)
                for q in range(Q):
                    last = nc.tensor.transpose(mask_tp[:, q, :], mask[:, t % MASKS, q:N:Q], ident_b[:, :])
                last.then_inc(s_transposed, 1)

            def rank_half(t, g, to):
                nc.tensor.matmul(to, rank_w[:, :], mask_t[:, t % 2, g * HALF:(g + 1) * HALF, :],
                                 start=True, stop=True).then_inc(s_ranked, 1)

            def count_tile(t, to):
                for q in range(Q):
                    last = nc.tensor.matmul(to[:, q:q + 1], mask_t[:, t % 2, q, :], ones[:, 0:1],
                                            start=True, stop=True)
                last.then_inc(s_counted, 1)

            def transpose_h(par, t):
                for k in range(H_PIECE):
                    last = nc.tensor.transpose(bank_b[:, k * P:(k + 1) * P], h[:, par, t * H_PIECE + k, :],
                                               ident_f[:, :])
                last.then_inc(s_h_tp, 1)

            def project(par, s, to):
                nc.tensor.matmul(to, ones[:, 0:P], bias_parts[:, :], start=True, stop=False)
                nc.tensor.matmul(to, h_t[:, par, s, :], w_sb[:, 0, :], start=False, stop=False)
                nc.tensor.matmul(to, agg[:, par, s:N:Q], w_sb[:, 1, :], start=False, stop=True).then_inc(s_proj, 1)

            def gather_level(par, buf, now):
                pe.wait_ge(s_onehot, now + buf + 1)
                for q in range(Q):
                    for part in range(PARTS):
                        last = nc.tensor.matmul(gathered[:, buf, q, :], h_parts[:, par, part, q, :],
                                                onehot[:, buf, q, :], start=(part == 0), stop=(part == PARTS - 1))
                last.then_inc(s_gathered, 1)

            pe.wait_ge(s_consts, N_CONSTS)
            for t in range(TILES + 1):
                if t >= 1:
                    pe.wait_ge(s_mask_t, t)
                if t < TILES:
                    transpose_tile(t, t)
                if t >= 1:
                    if t > RING:
                        pe.wait_ge(s_rank_sb, 2 * (t - RING))
                    for g in range(2):
                        rank_half(t - 1, g, gathered[:, (t - 1) % RING, g * HALF:(g + 1) * HALF, :])
                    if t >= 2:
                        pe.wait_ge(s_counts_sb, t - 1)
                    count_tile(t - 1, first_counts_ps)
            pe.wait_ge(s_rank_sb, 2 * TILES)

            def graph(b, par, rnd, pair):
                first, last = is_first(b), is_last(b)
                pe.wait_ge(s_lo, b + 1)
                for t in range(TILES):
                    u = TILES * (b + 1) + t
                    now = pe.snap(level)
                    gather_level(par, 0, now)
                    if (t == 0 and not first) or (t > 0 and not last):
                        pe.wait_ge(s_rank_sb, 2 * u - 1)
                        rank_half((t - 1) % TILES, 1, bank_b[:, :])
                    if not last:
                        pe.wait_ge(s_counts_sb, u)
                        transpose_tile(u, t)
                    gather_level(par, 1, now)
                    if t < H_PIECES:
                        if first and t == 0:
                            pe.wait_ge(s_counts_sb, TILES)
                        elif last and t > 0:
                            pe.wait_ge(s_h_t, H_PIECES * b + t)
                        else:
                            pe.wait_ge(s_rank_sb, 2 * u)
                        transpose_h(par, t)
                    gather_level(par, 2, now)
                    if not last:
                        pe.wait_ge(s_mask_t, u + 1)
                        if t < H_PIECES:
                            pe.wait_ge(s_h_t, H_PIECES * b + t + 1)
                        else:
                            pe.wait_ge(s_rank_sb, 2 * u)
                        rank_half(t, 0, bank_b[:, :])
                        count_tile(t, counts_ps)
                    if not first:
                        if t == 0:
                            pe.wait_ge(s_weights, 16)
                            pe.wait_ge(s_bias_parts, 1)
                            pe.wait_ge(s_agg, b)
                            pe.wait_ge(s_h_t, H_PIECES * b)
                        if last:
                            if t == 0:
                                pe.wait_ge(s_counts_sb, u)
                            else:
                                pe.wait_ge(s_relu, TILES * (b - 1) + t)
                        project(1 - par, t, projection)
                    pe.reg_add(level, level, RING)
                    if t == 0:
                        wait_alone(pe, s_levels, b + 1)
                        n_levels = load_numbers(nc.tensor, levels_int[0:1, par, :], MIN_LEVELS, SAMPLES)
                        rounds = pe.snap((sum(n_levels[1:], n_levels[0]) + (RING - 1)) // RING - TILES)
                    begin = pe.snap(rounds * t // TILES)
                    end = pe.snap(rounds * (t + 1) // TILES)
                    with pe.If(begin < end):
                        with pe.Fori(begin, end):
                            now = pe.snap(level)
                            for buf in range(RING):
                                gather_level(par, buf, now)
                            pe.reg_add(level, level, RING)

            over_graphs(pe, graph)
            pe.wait_ge(s_agg, NBATCH)
            pe.wait_ge(s_h_t, H_PIECES * NBATCH)
            pe.wait_ge(s_relu, TILES * LAST)
            for s in range(TILES):
                project(1, s, last_projection(s))


def kernel(x, adj, L0_gnn_W, L0_gnn_b):
    import numpy as np
    import concourse.bacc as bacc
    from concourse import mybir
    from concourse.bass_utils import run_bass_kernel_spmd

    nc = bacc.Bacc("TRN2", target_bir_lowering=False, num_devices=1)
    arrays, args = {}, []
    for name, a in (("x", x), ("adj", adj), ("w", L0_gnn_W), ("bias", L0_gnn_b)):
        a = np.ascontiguousarray(a)
        arrays[name] = a
        args.append(nc.dram_tensor(name, a.shape, mybir.dt.from_np(a.dtype), kind="ExternalInput").ap())
    args.append(nc.dram_tensor("out", arrays["x"].shape, mybir.dt.float32, kind="ExternalOutput").ap())
    gnn_layer(nc, *args)
    result = run_bass_kernel_spmd(nc, [arrays], core_ids=[0])
    return result.results[0]["out"]
```
